# Optimizing a Trainium2 kernel written in Bass

```python
import numpy as np
import jax
import jax.numpy as jnp

def _softmax(x, axis=-1):
    return jax.nn.softmax(x, axis=axis)

def _gelu(x):
    return jax.nn.gelu(x, approximate=True)

def _silu(x):
    return jax.nn.silu(x)

def _sigmoid(x):
    return jax.nn.sigmoid(x)

def _layernorm(x, axis=-1, eps=1e-05):
    m = jnp.mean(x, axis=axis, keepdims=True)
    v = jnp.var(x, axis=axis, keepdims=True)
    return (x - m) / jnp.sqrt(v + eps)

def _scatter_add(tgt, idx, src, axis=0):
    return tgt.at[idx].add(src)

def _segment_sum(src, seg, n):
    return jax.ops.segment_sum(src, seg, n)
kernel_name = 'mk_gnn_preln_d1_gnn_r32_94146b'

def setup_inputs(seed: int=0):
    np.random.seed(seed)
    _w = jnp.asarray

    def _rec_inputs():
        import jax
        import jax.numpy as jnp
        _gk = jax.random.key(seed)
        x = -0.000202 + 1 * jax.random.normal(jax.random.fold_in(_gk, 1), (3125, 128), jnp.float32)
        src = jax.random.randint(jax.random.fold_in(_gk, 2), (50000,), 0, 3125, jnp.int32)
        dst = jnp.minimum((3125 * jax.random.uniform(jax.random.fold_in(_gk, 3), (50000,)) ** 2.0).astype(jnp.int32), 99999)
        _o = jnp.argsort(dst, stable=True)
        src = src[_o]
        dst = dst[_o]
        edge_attr_64 = 0.000189758 + 1.00013 * jax.random.normal(jax.random.fold_in(_gk, 11), (50000, 64), jnp.float32)
        return (x, src, dst, edge_attr_64)
    x, src, dst, edge_attr_64 = _rec_inputs()

    def _L0_gnn_setup():
        import jax, jax.numpy as jnp
        import numpy as np
        N_NODES = 50000
        N_EDGES = 25000
        F_NODE = 128
        F_EDGE = 64
        Z_DIM = 2 * F_NODE + F_EDGE
        BN_EPS = 1e-05

        def _params(key):
            ks = jax.random.split(key, 16)
            s = 1.0 / np.sqrt(Z_DIM)
            p = {}
            for li, k4 in zip((1, 2), (ks[:8], ks[8:])):
                p[f'Wf{li}'] = jax.random.uniform(k4[0], (Z_DIM, F_NODE), jnp.float32, -s, s)
                p[f'bf{li}'] = jax.random.uniform(k4[1], (F_NODE,), jnp.float32, -s, s)
                p[f'Ws{li}'] = jax.random.uniform(k4[2], (Z_DIM, F_NODE), jnp.float32, -s, s)
                p[f'bs{li}'] = jax.random.uniform(k4[3], (F_NODE,), jnp.float32, -s, s)
                p[f'gamma{li}'] = jnp.ones((F_NODE,), jnp.float32)
                p[f'beta{li}'] = jnp.zeros((F_NODE,), jnp.float32)
                p[f'rmean{li}'] = jax.random.normal(k4[4], (F_NODE,), jnp.float32) * 0.1
                p[f'rvar{li}'] = jax.random.uniform(k4[5], (F_NODE,), jnp.float32, 0.5, 1.5)
            return p

        def _cgconv(x, src, dst, edge_attr, Wf, bf, Ws, bs, gamma, beta, rmean, rvar):
            z = jnp.concatenate([x[dst], x[src], edge_attr], axis=-1)
            msg = jax.nn.sigmoid(z @ Wf + bf) * jax.nn.softplus(z @ Ws + bs)
            n = x.shape[0]
            summed = jax.ops.segment_sum(msg, dst, num_segments=n)
            cnt = jax.ops.segment_sum(jnp.ones((dst.shape[0],), x.dtype), dst, num_segments=n)
            out = summed / jnp.maximum(cnt, 1.0)[:, None]
            out = (out - rmean) * jax.lax.rsqrt(rvar + BN_EPS) * gamma + beta
            return out + x
        key = jax.random.key(seed)
        k1, k2, k3, kp = jax.random.split(key, 4)
        inp = {'x': jax.random.normal(k1, (N_NODES, F_NODE), jnp.float32), 'edge_index': jax.random.randint(k2, (2, N_EDGES), 0, N_NODES, jnp.int64), 'edge_attr': jax.random.normal(k3, (N_EDGES, F_EDGE), jnp.float32)}
        inp.update(_params(kp))
        return inp
    _L0_gnn_all = _L0_gnn_setup()
    _L0_gnn_in = {k: v for k, v in _L0_gnn_all.items() if k in ('Wf1', 'bf1', 'Ws1', 'bs1', 'gamma1', 'beta1', 'rmean1', 'rvar1', 'Wf2', 'bf2', 'Ws2', 'bs2', 'gamma2', 'beta2', 'rmean2', 'rvar2')}
    del _L0_gnn_all
    return {'x': x, 'src': src, 'dst': dst, 'edge_attr_64': edge_attr_64, 'L0_gnn_Wf1': _L0_gnn_in['Wf1'], 'L0_gnn_bf1': _L0_gnn_in['bf1'], 'L0_gnn_Ws1': _L0_gnn_in['Ws1'], 'L0_gnn_bs1': _L0_gnn_in['bs1'], 'L0_gnn_gamma1': _L0_gnn_in['gamma1'], 'L0_gnn_beta1': _L0_gnn_in['beta1'], 'L0_gnn_rmean1': _L0_gnn_in['rmean1'], 'L0_gnn_rvar1': _L0_gnn_in['rvar1'], 'L0_gnn_Wf2': _L0_gnn_in['Wf2'], 'L0_gnn_bf2': _L0_gnn_in['bf2'], 'L0_gnn_Ws2': _L0_gnn_in['Ws2'], 'L0_gnn_bs2': _L0_gnn_in['bs2'], 'L0_gnn_gamma2': _L0_gnn_in['gamma2'], 'L0_gnn_beta2': _L0_gnn_in['beta2'], 'L0_gnn_rmean2': _L0_gnn_in['rmean2'], 'L0_gnn_rvar2': _L0_gnn_in['rvar2']}

def reference(x, src, dst, edge_attr_64, L0_gnn_Wf1, L0_gnn_bf1, L0_gnn_Ws1, L0_gnn_bs1, L0_gnn_gamma1, L0_gnn_beta1, L0_gnn_rmean1, L0_gnn_rvar1, L0_gnn_Wf2, L0_gnn_bf2, L0_gnn_Ws2, L0_gnn_bs2, L0_gnn_gamma2, L0_gnn_beta2, L0_gnn_rmean2, L0_gnn_rvar2):
    import jax
    import jax.numpy as jnp

    def _L0_gnn_ref(x, edge_index, edge_attr, Wf1, bf1, Ws1, bs1, gamma1, beta1, rmean1, rvar1, Wf2, bf2, Ws2, bs2, gamma2, beta2, rmean2, rvar2):
        import jax, jax.numpy as jnp
        import numpy as np
        N_NODES = 50000
        N_EDGES = 25000
        F_NODE = 128
        F_EDGE = 64
        Z_DIM = 2 * F_NODE + F_EDGE
        BN_EPS = 1e-05

        def _params(key):
            ks = jax.random.split(key, 16)
            s = 1.0 / np.sqrt(Z_DIM)
            p = {}
            for li, k4 in zip((1, 2), (ks[:8], ks[8:])):
                p[f'Wf{li}'] = jax.random.uniform(k4[0], (Z_DIM, F_NODE), jnp.float32, -s, s)
                p[f'bf{li}'] = jax.random.uniform(k4[1], (F_NODE,), jnp.float32, -s, s)
                p[f'Ws{li}'] = jax.random.uniform(k4[2], (Z_DIM, F_NODE), jnp.float32, -s, s)
                p[f'bs{li}'] = jax.random.uniform(k4[3], (F_NODE,), jnp.float32, -s, s)
                p[f'gamma{li}'] = jnp.ones((F_NODE,), jnp.float32)
                p[f'beta{li}'] = jnp.zeros((F_NODE,), jnp.float32)
                p[f'rmean{li}'] = jax.random.normal(k4[4], (F_NODE,), jnp.float32) * 0.1
                p[f'rvar{li}'] = jax.random.uniform(k4[5], (F_NODE,), jnp.float32, 0.5, 1.5)
            return p

        def _cgconv(x, src, dst, edge_attr, Wf, bf, Ws, bs, gamma, beta, rmean, rvar):
            z = jnp.concatenate([x[dst], x[src], edge_attr], axis=-1)
            msg = jax.nn.sigmoid(z @ Wf + bf) * jax.nn.softplus(z @ Ws + bs)
            n = x.shape[0]
            summed = jax.ops.segment_sum(msg, dst, num_segments=n)
            cnt = jax.ops.segment_sum(jnp.ones((dst.shape[0],), x.dtype), dst, num_segments=n)
            out = summed / jnp.maximum(cnt, 1.0)[:, None]
            out = (out - rmean) * jax.lax.rsqrt(rvar + BN_EPS) * gamma + beta
            return out + x
        src, dst = (edge_index[0], edge_index[1])
        x = _cgconv(x, src, dst, edge_attr, Wf1, bf1, Ws1, bs1, gamma1, beta1, rmean1, rvar1)
        x = _cgconv(x, src, dst, edge_attr, Wf2, bf2, Ws2, bs2, gamma2, beta2, rmean2, rvar2)
        return x
    edge_index = jnp.stack([src, dst])
    h = jnp.maximum(_layernorm(x, axis=-1), 0.0)
    x = x + _L0_gnn_ref(h, edge_index, edge_attr_64, L0_gnn_Wf1, L0_gnn_bf1, L0_gnn_Ws1, L0_gnn_bs1, L0_gnn_gamma1, L0_gnn_beta1, L0_gnn_rmean1, L0_gnn_rvar1, L0_gnn_Wf2, L0_gnn_bf2, L0_gnn_Ws2, L0_gnn_bs2, L0_gnn_gamma2, L0_gnn_beta2, L0_gnn_rmean2, L0_gnn_rvar2)
    return x

_drawn_inputs = setup_inputs


def setup_inputs(seed=0):
    import zlib

    import numpy as np

    out = dict(_drawn_inputs(seed))
    spreads = {'L0_gnn_gamma1': (1.0, 0.2),
     'L0_gnn_beta1': (0.0, 0.1),
     'L0_gnn_gamma2': (1.0, 0.2),
     'L0_gnn_beta2': (0.0, 0.1)}
    factors = {'edge_attr_64': 2.746,
     'L0_gnn_bf1': 8.0,
     'L0_gnn_bs1': 8.0,
     'L0_gnn_bf2': 8.0,
     'L0_gnn_bs2': 8.0}
    for name, (base, spread) in spreads.items():
        noise = np.random.default_rng([zlib.crc32(name.encode()), seed]).standard_normal(out[name].shape)
        drawn = base * np.exp(spread * noise) if base else spread * noise
        out[name] = jnp.asarray(drawn.astype(out[name].dtype))
    for name, factor in factors.items():
        out[name] = (out[name] * factor).astype(out[name].dtype)
    return out
```

```python
from contextlib import ExitStack

import numpy as np

import concourse.bass as bass
from concourse import mybir

P = 128
F = 128
FE = 64
Z = 2 * F
N_NODES = 3125
CH = -(-N_NODES // P)
NP = CH * P
N_EDGES = 50000
TQ = 4
QE = TQ * P
QUADS = -(-N_EDGES // QE)
EP = QUADS * QE
TILES = EP // P
GQ = 2
TG = TQ // GQ
GROUPS = QUADS * GQ
W = 64
SL = 4
LOG_EXP = "natural_log_exp_and_others"
TP = 5
TURN_N = CH // TP
LAST = N_NODES // P
LN_EPS = 1e-5
BN_EPS = 1e-5
CAP = 40.0

ALU = mybir.AluOpType
ACT = mybir.ActivationFunctionType
F32 = mybir.dt.float32
BF16 = mybir.dt.bfloat16
I32 = mybir.dt.int32
AX = mybir.AxisListType
RMAX = bass.bass_isa.ReduceOp.max

FORCE_GENERAL = False


def build(nc, x, src_cols, dst_cols, dst_row, dst_first, edge_t, weights, out):
    ctx = ExitStack()
    with ctx:
        def sb(name, shape, dt=F32):
            return ctx.enter_context(nc.sbuf_tensor(name, shape, dt))

        def ps(name, shape, dt=F32):
            return ctx.enter_context(nc.psum_tensor(name, shape, dt))

        def sem(name):
            return ctx.enter_context(nc.semaphore(name))

        a_table = nc.dram_tensor("a_table", (NP, Z), F32).ap()
        b_table = nc.dram_tensor("b_table", (NP, Z), F32).ap()

        x_rows = sb("x_rows", [P, CH, F])
        h_rows = sb("h_rows", [P, CH, F])
        h_t = sb("h_t", [P, NP])
        acc = sb("acc", [P, 2, NP])
        inv_cnt = sb("inv_cnt", [P, NP])
        mean_t = sb("mean_t", [P, NP])
        sq = mean_t[:].rearrange("p (c f) -> p c f", f=F)
        mean = sb("mean", [P, CH])
        var = sb("var", [P, CH])
        rstd = sb("rstd", [P, CH])
        ident = sb("ident", [P, P])
        ones_bf = sb("ones_bf", [P, P], BF16)
        w_node = sb("w_node", [P, 2, 2, 2, F])
        w_edge = sb("w_edge", [P, 2, 2, F])
        bias = sb("bias", [P, 2, 2, 2, F])
        bn = sb("bn", [P, 2, 4])
        bn_scale = sb("bn_scale", [P, 2])
        bn_shift = sb("bn_shift", [P, 2])
        bn_tmp = sb("bn_tmp", [P, 2, 2])
        tab = sb("tab", [P, TP, 2, Z])

        src_i = sb("src_i", [P, TILES + 1], I32)
        dst_i = sb("dst_i", [P, TILES + 1], I32)
        first_i = sb("first_i", [P, GROUPS], I32)
        first_f = sb("first_f", [P, GROUPS])
        dst_f = sb("dst_f", [P, TILES])
        rel = sb("rel", [P, TILES])
        outside = sb("outside", [P, TILES])
        outside2 = sb("outside2", [P, TILES])
        worst = sb("worst", [P, 1])
        worst_all = sb("worst_all", [P, 1])
        flag = sb("flag", [P, 1], I32)
        target = sb("target", [W, GROUPS])
        iota_i = sb("iota_i", [P, P], I32)
        iota_f = sb("iota_f", [P, P])
        part_i = sb("part_i", [P, 1], I32)
        part_f = sb("part_f", [P, 1])

        left = sb("left", [P, SL, QE])
        right = sb("right", [P, SL, GQ, Z])
        dst_b = sb("dst_b", [W, SL, QE], I32)
        idx = sb("idx", [P, SL, TQ], I32)
        gath = sb("gath", [P, SL, TQ, Z])
        hot = sb("hot", [P, SL, TQ, W])
        z = sb("z", [P, 2, TQ, Z])
        lnz = sb("lnz", [P, 2, TQ, Z])
        soft = sb("soft", [P, 2, TQ, F])
        gate = sb("gate", [P, 2, TQ, F])
        msg = sb("msg", [P, 2, TQ, F])
        rel_w = sb("rel_w", [P, 1])
        hot_w = sb("hot_w", [P, P])

        ps_z = [ps(f"ps_z{i}", [P, TQ, Z]) for i in range(2)]
        ps_s = [ps(f"ps_s{i}", [P, 512]) for i in range(2)]
        ps_n = ps("ps_n", [P, 512])
        bank = [ps_z[0][:, 0:2, :], ps_z[0][:, 2:4, :], ps_z[1][:, 0:2, :], ps_z[1][:, 2:4, :],
                ps_n[:, :].rearrange("p (s z) -> p s z", s=2)]

        x_in = sem("x_in")
        idx_in = sem("idx_in")
        w_in = sem("w_in")
        iota_ready = sem("iota_ready")
        ident_ready = sem("ident_ready")
        acc_zero = sem("acc_zero")
        prep = sem("prep")
        var_ready = sem("var_ready")
        root_ready = sem("root_ready")
        h_ready = sem("h_ready")
        turned = sem("turned")
        h_t_ready = sem("h_t_ready")
        w_ready = sem("w_ready")
        worst_ready = sem("worst_ready")
        worst_spread = sem("worst_spread")
        flag_ready = sem("flag_ready")
        index_ready = sem("index_ready")
        right_ready = sem("right_ready")
        tab_mm = sem("tab_mm")
        tab_rows = sem("tab_rows")
        tab_out = [sem(f"tab_out{i}") for i in range(TP)]
        edge_in = [sem(f"edge_in{i}") for i in range(SL)]
        dst_in = [sem(f"dst_in{i}") for i in range(SL)]
        win_in = [sem(f"win_in{i}") for i in range(SL)]
        idx_set = sem("idx_set")
        gath_in = [sem(f"gath_in{i}") for i in range(SL)]
        hots_ready = sem("hots_ready")
        z_mm = sem("z_mm")
        z_ready = sem("z_ready")
        exp_ready = sem("exp_ready")
        ln_ready = sem("ln_ready")
        soft_ready = sem("soft_ready")
        gate_ready = sem("gate_ready")
        msg_ready = sem("msg_ready")
        sums_mm = sem("sums_mm")
        acc_done = sem("acc_done")
        g_edge_in = sem("g_edge_in")
        g_rows_in = sem("g_rows_in")
        g_idx_set = sem("g_idx_set")
        g_z_mm = sem("g_z_mm")
        g_zb = sem("g_zb")
        g_z = sem("g_z")
        g_exp = sem("g_exp")
        g_ln = sem("g_ln")
        g_soft = sem("g_soft")
        g_gate = sem("g_gate")
        g_msg = sem("g_msg")
        g_rel = sem("g_rel")
        g_hot = sem("g_hot")
        g_sums = sem("g_sums")
        g_acc = sem("g_acc")
        edges_done = sem("edges_done")
        out_ready = sem("out_ready")
        out_sent = sem("out_sent")

        IDX_LOADS, W_LOADS = 3 * 16, 2 * (4 + 2 + 2 + 4) * 16
        TURNS = QUADS // SL
        REST = QUADS % SL

        def used(u):
            return TURNS + (1 if u < REST else 0)

        def steps(eng, step, ahead, behind):
            lo = 1
            hi = TURNS - 1
            for n in range(-ahead, lo * SL):
                step(n // SL, n % SL)
            with eng.Fori(0, hi - lo) as i:
                for u in range(SL):
                    step(i + lo, u)
            for n in range(hi * SL, QUADS + behind):
                step(n // SL, n % SL)

        def first_then_rest(eng, body, n):
            body(0)
            with eng.Fori(1, n) as i:
                body(i)

        def live(turn, u, shift=0):
            return not isinstance(turn, int) or 0 <= SL * turn + u + shift < QUADS

        def at(turn, u, shift):
            m = u + shift
            return (turn + m // SL if m // SL else turn), m % SL

        def first_row(eng, g):
            return eng.value_load(first_i[0:1, bass.ds(g, 1)], min_val=0, max_val=NP - W)

        def choose(eng, fast, general):
            f = eng.value_load(flag[0:1, 0:1], min_val=0, max_val=1)
            with eng.If(f == 0):
                fast()
            with eng.Else():
                general()

        block = ctx.enter_context(nc.Block())

        @block.sync
        def _(sp):
            sp.dma_start(x_rows[:], x.rearrange("(c p) f -> p c f", p=P)).then_inc(x_in, 16)
            sp.dma_start(dst_i[:], dst_cols).then_inc(idx_in, 16)
            sp.dma_start(src_i[:], src_cols).then_inc(idx_in, 16)
            sp.dma_start(first_i[:], dst_first[None, :].to_broadcast((P, GROUPS))).then_inc(idx_in, 16)
            for l in range(2):
                for j, half in enumerate(("Wf", "Ws")):
                    w = weights[f"{half}{l + 1}"]
                    sp.dma_start(w_node[:, l, 0, j, :], w[0:F, :]).then_inc(w_in, 16)
                    sp.dma_start(w_node[:, l, 1, j, :], w[F:2 * F, :]).then_inc(w_in, 16)
                    sp.dma_start(w_edge[P - FE:P, l, j, :], w[2 * F:2 * F + FE, :]).then_inc(w_in, 16)
                    b = weights[("bf", "bs")[j] + str(l + 1)]
                    sp.dma_start(bias[:, l, 0, j, :], b[None, :].to_broadcast((P, F))).then_inc(w_in, 16)
                for k, name in enumerate(("gamma", "beta", "rmean", "rvar")):
                    sp.dma_start(bn[:, l, k:k + 1], weights[f"{name}{l + 1}"][:, None]).then_inc(w_in, 16)

            for l in range(2):
                with sp.Fori(0, TURN_N) as i:
                    for u in range(TP):
                        c = i * TP + u
                        sp.wait_ge(tab_rows, l * CH + i * TP + u + 1)
                        sp.dma_start(a_table[bass.ds(c * P, P), :], tab[:, u, 0, :]).then_inc(tab_out[u], 16)
                        sp.dma_start(b_table[bass.ds(c * P, P), :], tab[:, u, 1, :]).then_inc(tab_out[u], 16)
                for u in range(TP):
                    sp.wait_ge(tab_out[u], 32 * (l + 1) * (TURN_N))

                def load(turn, u):
                    if not live(turn, u):
                        return
                    n = turn * SL + u
                    if not isinstance(turn, int) or turn > 0:
                        sp.wait_ge(z_mm, n + l * QUADS - SL + 1)
                        sp.wait_ge(hots_ready, n + l * QUADS - SL + 1)
                    sp.dma_start(dst_b[:, u, :], dst_row[None, bass.ds(n * QE, QE)].to_broadcast((W, QE)))\
                        .then_inc(dst_in[u], 16)
                    sp.dma_start(left[W:P, u, :], edge_t[:, bass.ds(n * QE, QE)]).then_inc(edge_in[u], 16)
                    for k in range(GQ):
                        row = first_row(sp, n * GQ + k)
                        sp.dma_start(right[0:W, u, k, :], a_table[bass.ds(row, W), :]).then_inc(win_in[u], 16)

                def fast():
                    steps(sp, load, 0, 0)

                def general():
                    def tile(t):
                        if l or not isinstance(t, int):
                            sp.wait_ge(g_z_mm, t + l * TILES)
                        sp.dma_start(left[W:P, 0, 0:P], edge_t[:, bass.ds(t * P, P)]).then_inc(g_edge_in, 16)

                    first_then_rest(sp, tile, TILES)

                if l == 0:
                    sp.wait_ge(idx_in, IDX_LOADS)
                    sp.wait_ge(flag_ready, 1)
                choose(sp, fast, general)

            for i in range(TURN_N):
                c = i * TP
                k = min(TP, N_NODES // P - c)
                sp.wait_ge(out_ready, i + 1)
                sp.dma_start(out[c * P:(c + k) * P, :].rearrange("(c p) f -> p c f", p=P),
                             h_rows[:, c:c + k, :]).then_inc(out_sent, 16)
            sp.dma_start(out[LAST * P:N_NODES, :], h_rows[0:N_NODES - LAST * P, LAST, :]).then_inc(out_sent, 16)
            sp.wait_ge(out_sent, 16 * (TURN_N + 1))

        @block.gpsimd
        def _(pool):
            nc.gpsimd.memset(ident[:], 0.0).then_inc(iota_ready, 1)
            nc.gpsimd.iota(iota_i[:], pattern=[[1, P]], base=0, channel_multiplier=0).then_inc(iota_ready, 1)
            nc.gpsimd.iota(part_i[:], pattern=[[0, 1]], base=0, channel_multiplier=1).then_inc(iota_ready, 1)
            nc.gpsimd.memset(ones_bf[:], 1.0).then_inc(iota_ready, 1)
            pool.wait_ge(iota_ready, 4)
            nc.gpsimd.affine_select(out=ident[:], in_=ident[:], compare_op=ALU.not_equal, fill=1.0, base=0,
                                    pattern=[[-1, P]], channel_multiplier=1).then_inc(ident_ready, 1)
            nc.gpsimd.memset(acc[:], 0.0).then_inc(acc_zero, 1)
            pool.wait_ge(worst_ready, 1)
            nc.gpsimd.partition_all_reduce(worst_all[:], worst[:], P, RMAX).then_inc(worst_spread, 1)
            pool.wait_ge(idx_in, IDX_LOADS)
            for l in range(2):
                for u in range(TP):
                    pool.wait_ge(tab_out[u], 32 * (l + 1) * (TURN_N))

                def gather(turn, u):
                    if live(turn, u):
                        m = turn * SL + u + l * QUADS
                        if not isinstance(turn, int) or turn > 0:
                            pool.wait_ge(z_ready, m - SL + 1)
                        pool.wait_ge(idx_set, m + 1)
                    if live(turn, u, 1):
                        t2, v = at(turn, u, 1)
                        n = t2 * SL + v
                        if live(t2, v, -SL):
                            pool.wait_ge(gath_in[v], 16 * TQ * (t2 + l * used(v)))
                        nc.gpsimd.tensor_copy(idx[:, v, :], src_i[:, bass.ds(n * TQ, TQ)]).then_inc(idx_set, 1)
                    if live(turn, u):
                        for k in range(TQ):
                            nc.gpsimd.indirect_dma_start(
                                gath[:, u, k, :], None, b_table,
                                bass.IndirectOffsetOnAxis(ap=idx[:, u, k:k + 1], axis=0)).then_inc(gath_in[u], 16)

                def fast():
                    steps(pool, gather, 1, 0)

                def general():
                    def indices(t, v):
                        nc.gpsimd.tensor_copy(idx[:, v, 0:1], dst_i[:, bass.ds(t, 1)]).then_inc(g_idx_set, 1)
                        nc.gpsimd.tensor_copy(idx[:, v, 1:2], src_i[:, bass.ds(t, 1)]).then_inc(g_idx_set, 1)

                    if l:
                        pool.wait_ge(g_idx_set, 2 * (TILES + 1))
                    indices(0, 0)
                    before = l * (TILES + 1)

                    def tiles(i):
                        for v in range(2):
                            t = i * 2 + v
                            m = t + l * TILES
                            if l or not isinstance(i, int) or v:
                                pool.wait_ge(g_z, m)
                            pool.wait_ge(g_idx_set, (t + before + 1) * 2)
                            indices(t + 1, 1 - v)
                            for k, table in enumerate((a_table, b_table)):
                                nc.gpsimd.indirect_dma_start(
                                    gath[:, 0, k, :], None, table,
                                    bass.IndirectOffsetOnAxis(ap=idx[:, v, k:k + 1], axis=0)).then_inc(g_rows_in, 16)

                    first_then_rest(pool, tiles, TILES // 2)

                if l == 0:
                    pool.wait_ge(flag_ready, 1)
                choose(pool, fast, general)
                if l == 0:
                    pool.wait_ge(h_t_ready, 2 * TURN_N)
                    nc.gpsimd.memset(acc[:, 0, :], 0.0).then_inc(acc_zero, 1)

        @block.tensor
        def _(pe):
            def turn_chunks(i, rows_of):
                for k in range(TP):
                    c = i * TP + k
                    t = nc.tensor.transpose(ps_z[i % 2][:].rearrange("p t z -> p (t z)")[:, k * P:(k + 1) * P],
                                            rows_of(c), ident[:])
                t.then_inc(turned, 1)

            pe.wait_ge(ident_ready, 1)
            pe.wait_ge(h_ready, 1)
            for i in range(TURN_N):
                if i >= 2:
                    pe.wait_ge(h_t_ready, i - 1)
                turn_chunks(i, lambda c: h_rows[:, c, :])
            pe.wait_ge(w_ready, 1)
            pe.wait_ge(iota_ready, 4)
            for l in range(2):
                for c in range(CH):
                    pe.wait_ge(h_t_ready, l * TURN_N + (c // TP + 1 if l else TURN_N))
                    if c >= TP:
                        pe.wait_ge(tab_rows, l * CH + c - TP + 1)
                    nc.tensor.matmul(bank[c % TP], h_t[:, c * P:(c + 1) * P],
                                     w_node[:, l, :, :, :].rearrange("p s j f -> p s (j f)"),
                                     start=True, stop=True).then_inc(tab_mm, 1)
                pe.wait_ge(tab_rows, (l + 1) * CH)

                def products(turn, u):
                    if live(turn, u):
                        m = turn * SL + u + l * QUADS
                        pe.wait_ge(hots_ready, m + 1)
                        pe.wait_ge(edge_in[u], 16 * (turn + l * used(u) + 1))
                        pe.wait_ge(win_in[u], 16 * GQ * (turn + l * used(u) + 1))
                        if live(turn, u, -2):
                            pe.wait_ge(z_ready, m - 1)
                        for k in range(TQ):
                            mm = nc.tensor.matmul(ps_z[u % 2][:, k, :], left[:, u, k * P:(k + 1) * P],
                                                  right[:, u, k // TG, :], start=True, stop=True)
                        mm.then_inc(z_mm, 1)
                    if live(turn, u, -2):
                        v = (u - 2) % SL
                        m = turn * SL + u - 2 + l * QUADS
                        pe.wait_ge(msg_ready, m + 1)
                        if live(turn, u, -4):
                            pe.wait_ge(acc_done, GQ * (m - 1))
                        sums = ps_s[v % 2][:, 0:GQ * 2 * W].rearrange("p (g s w) -> p g s w", g=GQ, s=2)
                        bits = hot[:, v, :, :].bitcast(BF16).rearrange("p t (w two) -> p t w two", two=2)
                        for g in range(GQ):
                            for k in range(TG):
                                mm = nc.tensor.matmul(sums[:, g, 0, :], msg[:, v % 2, g * TG + k, :],
                                                      hot[:, v, g * TG + k, :], start=k == 0, stop=k == TG - 1)
                            if l == 0:
                                for k in range(TG):
                                    mm = nc.tensor.matmul(sums[:, g, 1, :], ones_bf[:], bits[:, g * TG + k, :, 1],
                                                          start=k == 0, stop=k == TG - 1)
                        mm.then_inc(sums_mm, 1)

                def fast():
                    steps(pe, products, 0, 2)

                def general():
                    def tile(t):
                        m = t + l * TILES
                        pe.wait_ge(g_edge_in, 16 * (m + 1))
                        if l or not isinstance(t, int):
                            pe.wait_ge(g_zb, m)
                        nc.tensor.matmul(ps_z[0][:, 0, :], left[W:P, 0, 0:P], right[W:P, 0, 0, :],
                                         start=True, stop=True).then_inc(g_z_mm, 1)
                        with pe.Fori(0, CH) as w:
                            pe.wait_ge(g_msg, m + 1)
                            pe.wait_ge(g_hot, m * CH + w + 1)
                            bits = hot_w[:].bitcast(BF16).rearrange("p (w two) -> p w two", two=2)
                            mm = nc.tensor.matmul(ps_s[0][:, 0:P], msg[:, 0, 0, :], hot_w[:],
                                                  start=True, stop=True)
                            if l == 0:
                                mm = nc.tensor.matmul(ps_s[0][:, P:2 * P], ones_bf[:], bits[:, :, 1],
                                                      start=True, stop=True)
                            mm.then_inc(g_sums, 1)

                    first_then_rest(pe, tile, TILES)

                pe.wait_ge(right_ready, l + 1)
                if l == 0:
                    pe.wait_ge(flag_ready, 1)
                choose(pe, fast, general)

            for i in range(TURN_N):
                pe.wait_ge(h_t_ready, 2 * TURN_N + i + 1)
                if i >= 2:
                    pe.wait_ge(out_ready, i - 1)
                turn_chunks(i, lambda c: h_t[:, c * P:(c + 1) * P])

        @block.scalar
        def _(act):
            act.wait_ge(var_ready, 1)
            nc.scalar.activation(rstd[:], var[:], ACT.Sqrt).then_inc(root_ready, 1)
            act.wait_ge(var_ready, 2)
            nc.scalar.activation(bn_tmp[:, :, 1], bn_tmp[:, :, 0], ACT.Sqrt).then_inc(root_ready, 1)
            act.preload_act_table_set(LOG_EXP)
            for l in range(2):
                def logs(turn, u):
                    if not live(turn, u):
                        return
                    h = u % 2
                    m = turn * SL + u + l * QUADS
                    act.wait_ge(z_ready, m + 1)
                    if live(turn, u, -2):
                        act.wait_ge(soft_ready, m - 1)
                    nc.scalar.activation(lnz[:, h], z[:, h], ACT.Exp).then_inc(exp_ready, 1)
                    act.wait_ge(exp_ready, m + 1)
                    nc.scalar.activation(lnz[:, h], lnz[:, h], ACT.Ln, bias=1.0).then_inc(ln_ready, 1)
                    act.wait_ge(ln_ready, m + 1)
                    if live(turn, u, -2):
                        act.wait_ge(msg_ready, m - 1)
                    nc.scalar.activation(gate[:, h], lnz[:, h, :, 0:F], ACT.Exp, scale=-1.0).then_inc(gate_ready, 1)

                def fast():
                    steps(act, logs, 0, 0)

                def general():
                    def tile(t):
                        m = t + l * TILES
                        act.wait_ge(g_z, m + 1)
                        nc.scalar.activation(lnz[:, 0, 0], z[:, 0, 0], ACT.Exp).then_inc(g_exp, 1)
                        act.wait_ge(g_exp, m + 1)
                        nc.scalar.activation(lnz[:, 0, 0], lnz[:, 0, 0], ACT.Ln, bias=1.0).then_inc(g_ln, 1)
                        act.wait_ge(g_ln, m + 1)
                        nc.scalar.activation(gate[:, 0, 0], lnz[:, 0, 0, 0:F], ACT.Exp, scale=-1.0)\
                            .then_inc(g_gate, 1)

                    first_then_rest(act, tile, TILES)

                if l == 0:
                    act.wait_ge(flag_ready, 1)
                choose(act, fast, general)

        @block.vector
        def _(dve):
            done = [0]

            def link(ins):
                done[0] += 1
                ins.then_inc(prep, 1)
                dve.wait_ge(prep, done[0])

            dve.wait_ge(idx_in, IDX_LOADS)
            dve.wait_ge(iota_ready, 4)
            nc.vector.tensor_copy(iota_f[:], iota_i[:])
            nc.vector.tensor_copy(part_f[:], part_i[:])
            nc.vector.tensor_copy(first_f[:], first_i[:])
            link(nc.vector.tensor_copy(dst_f[:], dst_i[:, 0:TILES]))
            nc.vector.tensor_scalar(target[:], first_f[0:W, :], part_f[0:W, :], None, ALU.add)
            link(nc.vector.tensor_tensor(rel[:].rearrange("p (g t) -> p g t", t=TG),
                                         dst_f[:].rearrange("p (g t) -> p g t", t=TG),
                                         first_f[:].unsqueeze(2).to_broadcast((P, GROUPS, TG)), ALU.subtract))
            link(nc.vector.tensor_scalar(outside[:], rel[:], 0.0, None, ALU.is_lt))
            link(nc.vector.scalar_tensor_tensor(outside2[:], rel[:], W - 1.0, outside[:], ALU.is_gt, ALU.max))
            if FORCE_GENERAL:
                link(nc.vector.memset(outside2[:], 1.0))
            nc.vector.tensor_reduce(worst[:], outside2[:], AX.X, ALU.max).then_inc(worst_ready, 1)

            dve.wait_ge(x_in, 16)
            link(nc.vector.tensor_reduce(mean[:], x_rows[:], AX.X, ALU.add))
            link(nc.vector.tensor_scalar(mean[:], mean[:], 1.0 / F, None, ALU.mult))
            link(nc.vector.tensor_tensor(h_rows[:], x_rows[:], mean[:].unsqueeze(2).to_broadcast((P, CH, F)),
                                         ALU.subtract))
            link(nc.vector.tensor_tensor(sq[:], h_rows[:], h_rows[:], ALU.mult))
            link(nc.vector.tensor_reduce(var[:], sq[:], AX.X, ALU.add))
            nc.vector.tensor_scalar(var[:], var[:], 1.0 / F, LN_EPS, ALU.mult, ALU.add).then_inc(var_ready, 1)
            dve.wait_ge(root_ready, 1)
            link(nc.vector.reciprocal(rstd[:], rstd[:]))
            nc.vector.tensor_tensor(h_rows[:], h_rows[:], rstd[:].unsqueeze(2).to_broadcast((P, CH, F)),
                                    ALU.mult).then_inc(h_ready, 1)
            dve.wait_ge(worst_spread, 1)
            nc.vector.tensor_copy(flag[:], worst_all[:]).then_inc(flag_ready, 1)

            dve.wait_ge(w_in, W_LOADS)
            nc.vector.tensor_scalar(w_node[:, :, :, 0, :], w_node[:, :, :, 0, :], -1.0, None, ALU.mult)
            nc.vector.tensor_scalar(w_edge[W:P, :, 0, :], w_edge[W:P, :, 0, :], -1.0, None, ALU.mult)
            nc.vector.memset(bias[:, :, 1], 0.0)
            nc.vector.tensor_scalar(bias[:, :, 0, 0], bias[:, :, 0, 0], -1.0, None, ALU.mult)
            nc.vector.tensor_scalar(bn_tmp[:, :, 0], bn[:, :, 3], BN_EPS, None, ALU.add).then_inc(var_ready, 1)
            dve.wait_ge(root_ready, 2)
            link(nc.vector.reciprocal(bn_tmp[:, :, 1], bn_tmp[:, :, 1]))
            link(nc.vector.tensor_tensor(bn_scale[:], bn[:, :, 0], bn_tmp[:, :, 1], ALU.mult))
            link(nc.vector.tensor_tensor(bn_tmp[:, :, 0], bn[:, :, 2], bn_scale[:], ALU.mult))
            nc.vector.tensor_tensor(bn_shift[:], bn[:, :, 1], bn_tmp[:, :, 0], ALU.subtract).then_inc(w_ready, 1)
            dve.wait_ge(w_ready, 1)

            for i in range(TURN_N):
                dve.wait_ge(turned, i + 1)
                nc.vector.tensor_scalar(h_t[:, i * TP * P:(i + 1) * TP * P],
                                        ps_z[i % 2][:].rearrange("p t z -> p (t z)")[:, 0:TP * P],
                                        0.0, None, ALU.max).then_inc(h_t_ready, 1)

            for l in range(2):
                def table_rows(i):
                    for u in range(TP):
                        dve.wait_ge(tab_mm, l * CH + i * TP + u + 1)
                        if l or not isinstance(i, int):
                            dve.wait_ge(tab_out[u], 32 * (i + l * TURN_N))
                        nc.vector.tensor_tensor(tab[:, u], bank[u],
                                                bias[:, l].rearrange("p s j f -> p s (j f)"),
                                                ALU.add).then_inc(tab_rows, 1)

                first_then_rest(dve, table_rows, TURN_N)
                for j in range(SL):
                    mv = nc.vector.tensor_copy(
                        right[W:P, j], w_edge[W:P, l].rearrange("p j f -> p (j f)").unsqueeze(1)
                        .to_broadcast((FE, GQ, Z)))
                mv.then_inc(right_ready, 1)
                dve.wait_ge(acc_zero, l + 1)

                def elementwise(turn, u):
                    if live(turn, u):
                        h = u % 2
                        m = turn * SL + u + l * QUADS
                        dve.wait_ge(z_mm, m + 1)
                        dve.wait_ge(gath_in[u], 16 * TQ * (turn + l * used(u) + 1))
                        if live(turn, u, -2):
                            dve.wait_ge(soft_ready, m - 1)
                        nc.vector.tensor_tensor(z[:, h], ps_z[h][:], gath[:, u], ALU.add).then_inc(z_ready, 1)
                    if live(turn, u, -1):
                        h = (u - 1) % 2
                        m = turn * SL + u - 1 + l * QUADS
                        dve.wait_ge(ln_ready, m + 1)
                        if live(turn, u, -3):
                            dve.wait_ge(msg_ready, m - 1)
                        nc.vector.scalar_tensor_tensor(soft[:, h], lnz[:, h, :, F:Z], CAP, z[:, h, :, F:Z],
                                                       ALU.min, ALU.max).then_inc(soft_ready, 1)
                    if live(turn, u, 1):
                        t2, v = at(turn, u, 1)
                        n = t2 * SL + v
                        m = n + l * QUADS
                        dve.wait_ge(dst_in[v], 16 * (t2 + l * used(v) + 1))
                        if live(t2, v, -SL):
                            dve.wait_ge(z_mm, m - SL + 1)
                            dve.wait_ge(sums_mm, m - SL + 1)
                        for g in range(GQ):
                            nc.vector.tensor_scalar(
                                left[0:W, v, g * TG * P:(g + 1) * TG * P], dst_b[:, v, g * TG * P:(g + 1) * TG * P],
                                target[:, bass.ds(n * GQ + g, 1)], None, ALU.is_equal)
                        nc.vector.tensor_tensor(
                            hot[:, v], iota_f[:, 0:W].unsqueeze(1).to_broadcast((P, TQ, W)),
                            rel[:, bass.ds(n * TQ, TQ)].unsqueeze(2).to_broadcast((P, TQ, W)),
                            ALU.is_equal).then_inc(hots_ready, 1)
                    if live(turn, u, -1):
                        h = (u - 1) % 2
                        m = turn * SL + u - 1 + l * QUADS
                        dve.wait_ge(gate_ready, m + 1)
                        dve.wait_ge(soft_ready, m + 1)
                        if live(turn, u, -3):
                            dve.wait_ge(sums_mm, m - 1)
                        nc.vector.tensor_tensor(msg[:, h], gate[:, h], soft[:, h],
                                                ALU.mult).then_inc(msg_ready, 1)
                    if live(turn, u, -2):
                        h = u % 2
                        n = turn * SL + u - 2
                        m = n + l * QUADS
                        dve.wait_ge(sums_mm, m + 1)
                        sums = ps_s[h][:, 0:GQ * 2 * W].rearrange("p (g s w) -> p g s w", g=GQ, s=2)
                        k = 2 - l
                        for g in range(GQ):
                            row = first_row(dve, n * GQ + g)
                            if live(turn, u, -3) or g:
                                dve.wait_ge(acc_done, GQ * m + g)
                            there = acc[:, 0:k, bass.ds(row, W)]
                            nc.vector.tensor_tensor(there, there, sums[:, g, 0:k, :], ALU.add).then_inc(acc_done, 1)

                def fast():
                    steps(dve, elementwise, 1, 2)
                    dve.wait_ge(acc_done, GQ * QUADS * (l + 1))

                def general():
                    def tile(t):
                        m = t + l * TILES
                        dve.wait_ge(g_z_mm, m + 1)
                        dve.wait_ge(g_rows_in, 32 * (m + 1))
                        nc.vector.tensor_tensor(z[:, 0, 0], ps_z[0][:, 0], gath[:, 0, 0], ALU.add).then_inc(g_zb, 1)
                        dve.wait_ge(g_zb, m + 1)
                        nc.vector.tensor_tensor(z[:, 0, 0], z[:, 0, 0], gath[:, 0, 1], ALU.add).then_inc(g_z, 1)
                        dve.wait_ge(g_ln, m + 1)
                        nc.vector.scalar_tensor_tensor(soft[:, 0, 0], lnz[:, 0, 0, F:Z], CAP, z[:, 0, 0, F:Z],
                                                       ALU.min, ALU.max).then_inc(g_soft, 1)
                        nc.vector.tensor_copy(rel_w[:], dst_f[:, bass.ds(t, 1)]).then_inc(g_rel, 1)
                        dve.wait_ge(g_gate, m + 1)
                        dve.wait_ge(g_soft, m + 1)
                        if l or not isinstance(t, int):
                            dve.wait_ge(g_acc, m * CH)
                        nc.vector.tensor_tensor(msg[:, 0, 0], gate[:, 0, 0], soft[:, 0, 0],
                                                ALU.mult).then_inc(g_msg, 1)
                        with dve.Fori(0, CH) as w:
                            dve.wait_ge(g_rel, m * (CH + 1) + w + 1)
                            nc.vector.tensor_scalar(hot_w[:], iota_f[:], rel_w[:], None, ALU.is_equal)\
                                .then_inc(g_hot, 1)
                            dve.wait_ge(g_hot, m * CH + w + 1)
                            nc.vector.tensor_scalar(rel_w[:], rel_w[:], -float(P), None, ALU.add).then_inc(g_rel, 1)
                            dve.wait_ge(g_sums, m * CH + w + 1)
                            k = 2 - l
                            there = acc[:, 0:k, bass.ds(w * P, P)]
                            nc.vector.tensor_tensor(
                                there, there, ps_s[0][:, 0:k * P].rearrange("p (s w) -> p s w", s=k),
                                ALU.add).then_inc(g_acc, 1)

                    first_then_rest(dve, tile, TILES)
                    dve.wait_ge(g_acc, CH * TILES * (l + 1))

                if l == 0:
                    dve.wait_ge(flag_ready, 1)
                choose(dve, fast, general)

                for i in range(TURN_N):
                    c = slice(i * TP * P, (i + 1) * TP * P)
                    if l == 0:
                        link(nc.vector.tensor_scalar(inv_cnt[:, c], acc[:, 1, c], 1.0, None, ALU.max))
                        link(nc.vector.reciprocal(inv_cnt[:, c], inv_cnt[:, c]))
                    link(nc.vector.tensor_tensor(mean_t[:, c], acc[:, 0, c], inv_cnt[:, c], ALU.mult))
                    link(nc.vector.tensor_scalar(mean_t[:, c], mean_t[:, c], bn_scale[:, l:l + 1],
                                                 bn_shift[:, l:l + 1], ALU.mult, ALU.add))
                    nc.vector.tensor_tensor(h_t[:, c], h_t[:, c], mean_t[:, c], ALU.add).then_inc(h_t_ready, 1)
                    dve.wait_ge(h_t_ready, (l + 1) * TURN_N + i + 1)

            for i in range(TURN_N):
                dve.wait_ge(turned, TURN_N + i + 1)
                c = slice(i * TP, (i + 1) * TP)
                nc.vector.tensor_tensor(h_rows[:, c], x_rows[:, c],
                                        ps_z[i % 2][:].rearrange("p t z -> p (t z)")[:, 0:TP * P]
                                        .rearrange("p (c f) -> p c f", f=F), ALU.add).then_inc(out_ready, 1)


_WEIGHTS = [f"{n}{l}" for l in (1, 2) for n in ("Wf", "bf", "Ws", "bs", "gamma", "beta", "rmean", "rvar")]


def kernel(**inputs):
    import concourse.bacc as bacc
    from concourse.bass_utils import run_bass_kernel_spmd

    x = np.zeros((NP, F), np.float32)
    x[:N_NODES] = np.asarray(inputs["x"])
    src = np.zeros((EP,), np.int32)
    src[:N_EDGES] = np.asarray(inputs["src"])
    dst = np.full((EP,), N_NODES, np.int32)
    dst[:N_EDGES] = np.asarray(inputs["dst"])
    edge = np.zeros((EP, FE), np.float32)
    edge[:N_EDGES] = np.asarray(inputs["edge_attr_64"])
    cols = np.zeros((2, P, TILES + 1), np.int32)
    cols[0, :, :TILES] = src.reshape(TILES, P).T
    cols[1, :, :TILES] = dst.reshape(TILES, P).T
    arrays = {
        "x": x,
        "src_cols": cols[0],
        "dst_cols": cols[1],
        "dst_row": dst,
        "dst_first": np.ascontiguousarray(dst[::TG * P]),
        "edge_t": np.ascontiguousarray(edge.T),
    }
    for n in _WEIGHTS:
        arrays[n] = np.ascontiguousarray(np.asarray(inputs[f"L0_gnn_{n}"]))

    nc = bacc.Bacc("TRN2", target_bir_lowering=False, num_devices=1)
    aps = {n: nc.dram_tensor(f"in_{n}", a.shape, mybir.dt.from_np(a.dtype), kind="ExternalInput").ap()
           for n, a in arrays.items()}
    out = nc.dram_tensor("out", (N_NODES, F), F32, kind="ExternalOutput").ap()
    weights = {n: aps.pop(n) for n in _WEIGHTS}
    build(nc, weights=weights, out=out, **aps)
    r = run_bass_kernel_spmd(nc, [{f"in_{n}": a for n, a in arrays.items()}], core_ids=[0])
    return r.results[0]["out"]
```

```python
from contextlib import ExitStack

import numpy as np

import concourse.bass as bass
from concourse import mybir

P = 128
F = 128
FE = 64
Z = 2 * F
N_NODES = 3125
CH = -(-N_NODES // P)
NP = CH * P
N_EDGES = 50000
TQ = 4
QE = TQ * P
QUADS = -(-N_EDGES // QE)
EP = QUADS * QE
TILES = EP // P
GQ = 2
TG = TQ // GQ
GROUPS = QUADS * GQ
W = 64
SL = 4
LOG_EXP = "natural_log_exp_and_others"
NG = -(-CH // 4)
TP = 5
TURN_N = CH // TP
LAST = N_NODES // P
BNS = 6
LN_EPS = 1e-5
BN_EPS = 1e-5
CAP = 40.0

ALU = mybir.AluOpType
ACT = mybir.ActivationFunctionType
F32 = mybir.dt.float32
BF16 = mybir.dt.bfloat16
I32 = mybir.dt.int32
AX = mybir.AxisListType
RMAX = bass.bass_isa.ReduceOp.max

FORCE_GENERAL = False


def group(g):
    a, b = 4 * g, min(4 * g + 4, CH)
    return range(a, b), slice(a * P, b * P)


def build(nc, x, src_cols, dst_cols, dst_row, dst_first, edge_t, w_node_in, w_edge_in, bias_in, bn_in, out):
    ctx = ExitStack()
    with ctx:
        def sb(name, shape, dt=F32):
            return ctx.enter_context(nc.sbuf_tensor(name, shape, dt))

        def ps(name, shape, dt=F32):
            return ctx.enter_context(nc.psum_tensor(name, shape, dt))

        def sem(name):
            return ctx.enter_context(nc.semaphore(name))

        a_table = nc.dram_tensor("a_table", (NP, Z), F32).ap()
        b_table = nc.dram_tensor("b_table", (NP, Z), F32).ap()

        x_rows = sb("x_rows", [P, CH, F])
        h_rows = sb("h_rows", [P, CH, F])
        h_t = sb("h_t", [P, NP])
        acc = sb("acc", [P, 2, NP])
        mean_t = sb("mean_t", [P, NP])
        inv_cnt = sb("inv_cnt", [P, CH])
        stats = sb("stats", [P, CH, BNS])
        shift = sb("shift", [P, CH])
        tmp = sb("tmp", [P, CH])
        mean = sb("mean", [P, CH])
        var = sb("var", [P, CH])
        rstd = sb("rstd", [P, CH])
        ident = sb("ident", [P, P])
        ones_bf = sb("ones_bf", [P, P], BF16)
        w_node = sb("w_node", [P, 2, 2, 2, F])
        w_edge = sb("w_edge", [P, 2, 2, F])
        bias = sb("bias", [P, 2, 2, F])
        bn = sb("bn", [P, 2, 4])
        bn_scale = sb("bn_scale", [P, 2])
        bn_shift = sb("bn_shift", [P, 2])
        bn_tmp = sb("bn_tmp", [P, 2, 2])
        tab = sb("tab", [P, 2, TP, Z])

        src_i = sb("src_i", [P, TILES + 1], I32)
        dst_i = sb("dst_i", [P, TILES + 1], I32)
        first_i = sb("first_i", [P, GROUPS], I32)
        first_f = sb("first_f", [P, GROUPS])
        dst_f = sb("dst_f", [P, TILES])
        rel = sb("rel", [P, TILES])
        outside = sb("outside", [P, TILES])
        outside2 = sb("outside2", [P, TILES])
        worst = sb("worst", [P, 1])
        worst_all = sb("worst_all", [P, 1])
        flag = sb("flag", [P, 1], I32)
        target = sb("target", [W, GROUPS])
        iota_i = sb("iota_i", [P, P], I32)
        iota_f = sb("iota_f", [P, P])
        part_i = sb("part_i", [P, 1], I32)
        part_f = sb("part_f", [P, 1])

        left = sb("left", [P, SL, QE])
        right = sb("right", [P, SL, GQ, Z])
        dst_b = sb("dst_b", [W, SL, QE], I32)
        idx = sb("idx", [P, SL, TQ], I32)
        gath = sb("gath", [P, SL, TQ, Z])
        hot = sb("hot", [P, SL, TQ, W])
        z = sb("z", [P, 2, TQ, Z])
        lnz = sb("lnz", [P, 2, TQ, Z])
        soft = sb("soft", [P, 2, TQ, F])
        gate = sb("gate", [P, 2, TQ, F])
        msg = sb("msg", [P, 2, TQ, F])
        rel_w = sb("rel_w", [P, 1])
        hot_w = sb("hot_w", [P, P])

        ps_z = [ps(f"ps_z{i}", [P, TQ, Z]) for i in range(2)]
        ps_s = [ps(f"ps_s{i}", [P, 512]) for i in range(2)]
        ps_n = ps("ps_n", [P, 512])
        bank = [ps_z[i][:, 2 * j:2 * j + 2, :].rearrange("p t z -> p (t z)") for i in range(2) for j in range(2)]
        bank.append(ps_n[:, :])

        x_in = [sem(f"x_in{g}") for g in range(NG)]
        idx_in = sem("idx_in")
        w_in = sem("w_in")
        iota_ready = sem("iota_ready")
        ident_ready = sem("ident_ready")
        acc_zero = sem("acc_zero")
        prep = sem("prep")
        var_ready = sem("var_ready")
        root_ready = sem("root_ready")
        shift_ready = sem("shift_ready")
        h_ready = sem("h_ready")
        h_ready_act = sem("h_ready_act")
        turned = sem("turned")
        h_t_ready = sem("h_t_ready")
        w_ready = sem("w_ready")
        worst_ready = sem("worst_ready")
        worst_spread = sem("worst_spread")
        flag_ready = sem("flag_ready")
        index_ready = sem("index_ready")
        right_ready = sem("right_ready")
        tab_mm = sem("tab_mm")
        a_rows = sem("a_rows")
        b_rows = sem("b_rows")
        a_out = [sem(f"a_out{i}") for i in range(TP)]
        b_out = [sem(f"b_out{i}") for i in range(TP)]
        cnt_cols = sem("cnt_cols")
        inv_ready = sem("inv_ready")
        inv_spread = sem("inv_spread")
        mean_ready = sem("mean_ready")
        edge_in = [sem(f"edge_in{i}") for i in range(SL)]
        dst_in = [sem(f"dst_in{i}") for i in range(SL)]
        win_in = [sem(f"win_in{i}") for i in range(SL)]
        idx_set = sem("idx_set")
        gath_in = [sem(f"gath_in{i}") for i in range(SL)]
        hots_ready = sem("hots_ready")
        z_mm = sem("z_mm")
        z_ready = sem("z_ready")
        exp_ready = sem("exp_ready")
        ln_ready = sem("ln_ready")
        soft_ready = sem("soft_ready")
        gate_ready = sem("gate_ready")
        msg_ready = sem("msg_ready")
        sums_mm = sem("sums_mm")
        acc_done = sem("acc_done")
        g_edge_in = sem("g_edge_in")
        g_rows_in = sem("g_rows_in")
        g_idx_set = sem("g_idx_set")
        g_z_mm = sem("g_z_mm")
        g_zb = sem("g_zb")
        g_z = sem("g_z")
        g_exp = sem("g_exp")
        g_ln = sem("g_ln")
        g_soft = sem("g_soft")
        g_gate = sem("g_gate")
        g_msg = sem("g_msg")
        g_rel = sem("g_rel")
        g_hot = sem("g_hot")
        g_sums = sem("g_sums")
        g_acc = sem("g_acc")
        edges_done = sem("edges_done")
        out_ready = sem("out_ready")
        out_sent = sem("out_sent")

        IDX_LOADS, W_LOADS = 3 * 16, 4 * 16
        ACT_GROUPS = 3
        DVE_GROUPS = NG - ACT_GROUPS
        TURNS = QUADS // SL
        REST = QUADS % SL

        def used(u):
            return TURNS + (1 if u < REST else 0)

        def steps(eng, step, ahead, behind):
            lo = 1
            hi = TURNS - 1
            for n in range(-ahead, lo * SL):
                step(n // SL, n % SL)
            with eng.Fori(0, hi - lo) as i:
                for u in range(SL):
                    step(i + lo, u)
            for n in range(hi * SL, QUADS + behind):
                step(n // SL, n % SL)

        def first_then_rest(eng, body, n):
            body(0)
            with eng.Fori(1, n) as i:
                body(i)

        def live(turn, u, shift=0):
            return not isinstance(turn, int) or 0 <= SL * turn + u + shift < QUADS

        def at(turn, u, shift):
            m = u + shift
            return (turn + m // SL if m // SL else turn), m % SL

        def first_row(eng, g):
            return eng.value_load(first_i[0:1, bass.ds(g, 1)], min_val=0, max_val=NP - W)

        def choose(eng, fast, general):
            f = eng.value_load(flag[0:1, 0:1], min_val=0, max_val=1)
            with eng.If(f == 0):
                fast()
            with eng.Else():
                general()

        block = ctx.enter_context(nc.Block())

        @block.sync
        def _(sp):
            for g in range(NG):
                chunks, cols = group(g)
                sp.dma_start(x_rows[:, chunks.start:chunks.stop, :],
                             x[cols, :].rearrange("(c p) f -> p c f", p=P)).then_inc(x_in[g], 16)
            sp.dma_start(w_node[:].rearrange("p l s j f -> p (l s j f)"), w_node_in).then_inc(w_in, 16)
            sp.dma_start(w_edge[P - FE:P].rearrange("p l j f -> p (l j f)"), w_edge_in).then_inc(w_in, 16)
            sp.dma_start(bias[:].rearrange("p l j f -> p (l j f)"),
                         bias_in[None, :].to_broadcast((P, 2 * Z))).then_inc(w_in, 16)
            sp.dma_start(bn[:].rearrange("p l k -> p (l k)"), bn_in).then_inc(w_in, 16)
            sp.dma_start(dst_i[:], dst_cols).then_inc(idx_in, 16)
            sp.dma_start(first_i[:], dst_first[None, :].to_broadcast((P, GROUPS))).then_inc(idx_in, 16)
            sp.dma_start(src_i[:], src_cols).then_inc(idx_in, 16)

            for l in range(2):
                def edges(turn, u):
                    n = turn * SL + u
                    sp.dma_start(dst_b[:, u, :], dst_row[None, bass.ds(n * QE, QE)].to_broadcast((W, QE)))\
                        .then_inc(dst_in[u], 16)
                    sp.dma_start(left[W:P, u, :], edge_t[:, bass.ds(n * QE, QE)]).then_inc(edge_in[u], 16)

                def load(turn, u):
                    if not live(turn, u):
                        return
                    n = turn * SL + u
                    if not isinstance(turn, int) or turn > 0:
                        sp.wait_ge(z_mm, n + l * QUADS - SL + 1)
                        sp.wait_ge(hots_ready, n + l * QUADS - SL + 1)
                        edges(turn, u)
                    for k in range(GQ):
                        row = first_row(sp, n * GQ + k)
                        sp.dma_start(right[0:W, u, k, :], a_table[bass.ds(row, W), :]).then_inc(win_in[u], 16)

                def first_edges():
                    if l:
                        sp.wait_ge(z_mm, QUADS)
                    for u in range(SL):
                        edges(0, u)

                def nothing():
                    pass

                if l == 0:
                    sp.wait_ge(idx_in, IDX_LOADS)
                    sp.wait_ge(flag_ready, 1)
                choose(sp, first_edges, nothing)

                for s, (table, rows, sent) in enumerate(((b_table, b_rows, b_out), (a_table, a_rows, a_out))):
                    with sp.Fori(0, TURN_N) as i:
                        for u in range(TP):
                            sp.wait_ge(rows, l * CH + i * TP + u + 1)
                            sp.dma_start(table[bass.ds((i * TP + u) * P, P), :], tab[:, 1 - s, u, :])\
                                .then_inc(sent[u], 16)
                for u in range(TP):
                    sp.wait_ge(a_out[u], 16 * (l + 1) * TURN_N)

                def fast():
                    steps(sp, load, 0, 0)

                def general():
                    def tile(t):
                        if l or not isinstance(t, int):
                            sp.wait_ge(g_z_mm, t + l * TILES)
                        sp.dma_start(left[W:P, 0, 0:P], edge_t[:, bass.ds(t * P, P)]).then_inc(g_edge_in, 16)

                    first_then_rest(sp, tile, TILES)

                choose(sp, fast, general)

            for g in range(NG):
                chunks, cols = group(g)
                whole = min(chunks.stop, LAST) - chunks.start
                sp.wait_ge(out_ready, g + 1)
                if whole:
                    sp.dma_start(out[cols.start:cols.start + whole * P, :].rearrange("(c p) f -> p c f", p=P),
                                 h_rows[:, chunks.start:chunks.start + whole, :]).then_inc(out_sent, 16)
            sp.dma_start(out[LAST * P:N_NODES, :], h_rows[0:N_NODES - LAST * P, LAST, :]).then_inc(out_sent, 16)
            sp.wait_ge(out_sent, 16 * (-(-LAST // 4) + 1))

        @block.gpsimd
        def _(pool):
            nc.gpsimd.memset(ident[:], 0.0).then_inc(iota_ready, 1)
            nc.gpsimd.iota(iota_i[:], pattern=[[1, P]], base=0, channel_multiplier=0).then_inc(iota_ready, 1)
            nc.gpsimd.iota(part_i[:], pattern=[[0, 1]], base=0, channel_multiplier=1).then_inc(iota_ready, 1)
            nc.gpsimd.memset(ones_bf[:], 1.0).then_inc(iota_ready, 1)
            pool.wait_ge(iota_ready, 4)
            nc.gpsimd.affine_select(out=ident[:], in_=ident[:], compare_op=ALU.not_equal, fill=1.0, base=0,
                                    pattern=[[-1, P]], channel_multiplier=1).then_inc(ident_ready, 1)
            nc.gpsimd.memset(acc[:], 0.0).then_inc(acc_zero, 1)
            pool.wait_ge(worst_ready, 1)
            nc.gpsimd.partition_all_reduce(worst_all[:], worst[:], P, RMAX).then_inc(worst_spread, 1)
            pool.wait_ge(idx_in, IDX_LOADS)
            for l in range(2):
                for u in range(TP):
                    pool.wait_ge(b_out[u], 16 * (l + 1) * TURN_N)

                def gather(turn, u):
                    if live(turn, u):
                        m = turn * SL + u + l * QUADS
                        if not isinstance(turn, int) or turn > 0:
                            pool.wait_ge(z_ready, m - SL + 1)
                        pool.wait_ge(idx_set, m + 1)
                    if live(turn, u, 1):
                        t2, v = at(turn, u, 1)
                        n = t2 * SL + v
                        if live(t2, v, -SL):
                            pool.wait_ge(gath_in[v], 16 * TQ * (t2 + l * used(v)))
                        nc.gpsimd.tensor_copy(idx[:, v, :], src_i[:, bass.ds(n * TQ, TQ)]).then_inc(idx_set, 1)
                    if live(turn, u):
                        for k in range(TQ):
                            nc.gpsimd.indirect_dma_start(
                                gath[:, u, k, :], None, b_table,
                                bass.IndirectOffsetOnAxis(ap=idx[:, u, k:k + 1], axis=0)).then_inc(gath_in[u], 16)

                def fast():
                    steps(pool, gather, 1, 0)

                def general():
                    for u in range(TP):
                        pool.wait_ge(a_out[u], 16 * (l + 1) * TURN_N)

                    def indices(t, v):
                        nc.gpsimd.tensor_copy(idx[:, v, 0:1], dst_i[:, bass.ds(t, 1)]).then_inc(g_idx_set, 1)
                        nc.gpsimd.tensor_copy(idx[:, v, 1:2], src_i[:, bass.ds(t, 1)]).then_inc(g_idx_set, 1)

                    if l:
                        pool.wait_ge(g_idx_set, 2 * (TILES + 1))
                    indices(0, 0)
                    before = l * (TILES + 1)

                    def tiles(i):
                        for v in range(2):
                            t = i * 2 + v
                            m = t + l * TILES
                            if l or not isinstance(i, int) or v:
                                pool.wait_ge(g_z, m)
                            pool.wait_ge(g_idx_set, (t + before + 1) * 2)
                            indices(t + 1, 1 - v)
                            for k, table in enumerate((a_table, b_table)):
                                nc.gpsimd.indirect_dma_start(
                                    gath[:, 0, k, :], None, table,
                                    bass.IndirectOffsetOnAxis(ap=idx[:, v, k:k + 1], axis=0)).then_inc(g_rows_in, 16)

                    first_then_rest(pool, tiles, TILES // 2)

                if l == 0:
                    pool.wait_ge(flag_ready, 1)
                choose(pool, fast, general)
                if l == 0:
                    pool.wait_ge(h_t_ready, 2 * NG)
                    nc.gpsimd.memset(acc[:, 0, :], 0.0).then_inc(acc_zero, 1)

        @block.tensor
        def _(pe):
            def spread(l, g):
                m = l * NG + g
                if g >= 2:
                    pe.wait_ge(mean_ready, m - 1)
                for k, c in enumerate(group(g)[0]):
                    mm = nc.tensor.matmul(ps_s[g % 2][:, k * P:(k + 1) * P], inv_cnt[:, c:c + 1].to_broadcast((P, P)),
                                          ident[:], start=True, stop=True)
                mm.then_inc(inv_spread, 1)

            def transpose(g, part_of):
                for k, c in enumerate(group(g)[0]):
                    t = nc.tensor.transpose(bank[g % TP][:, k * P:(k + 1) * P], part_of(c), ident[:])
                t.then_inc(turned, 1)

            pe.wait_ge(ident_ready, 1)
            for g in range(NG):
                if g < DVE_GROUPS:
                    pe.wait_ge(h_ready, g + 1)
                else:
                    pe.wait_ge(h_ready_act, g - DVE_GROUPS + 1)
                if g >= TP:
                    pe.wait_ge(h_t_ready, g - TP + 1)
                transpose(g, lambda c: h_rows[:, c, :])
            pe.wait_ge(w_ready, 1)
            pe.wait_ge(iota_ready, 4)
            for l in range(2):
                for c in range(2 * CH):
                    s, c = (1, c) if c < CH else (0, c - CH)
                    if l and s and c % 4 == 0 and 1 <= c // 4 < NG - 1:
                        spread(0, c // 4 + 1)
                    pe.wait_ge(h_t_ready, l * NG + (c // 4 + 1 if l else NG))
                    if c >= TP:
                        pe.wait_ge((a_rows, b_rows)[s], l * CH + c - TP + 1)
                    elif s == 0:
                        pe.wait_ge(b_rows, (l + 1) * CH - TP + c + 1)
                    elif l == 0:
                        pe.wait_ge(h_t_ready, NG)
                    nc.tensor.matmul(bank[c % TP][:, 0:Z], h_t[:, c * P:(c + 1) * P],
                                     w_node[:, l, s, :, :].rearrange("p j f -> p (j f)"),
                                     start=True, stop=True).then_inc(tab_mm, 1)
                pe.wait_ge(a_rows, (l + 1) * CH)

                def products(turn, u):
                    if live(turn, u):
                        m = turn * SL + u + l * QUADS
                        pe.wait_ge(hots_ready, m + 1)
                        pe.wait_ge(edge_in[u], 16 * (turn + l * used(u) + 1))
                        pe.wait_ge(win_in[u], 16 * GQ * (turn + l * used(u) + 1))
                        if live(turn, u, -2):
                            pe.wait_ge(z_ready, m - 1)
                        for k in range(TQ):
                            mm = nc.tensor.matmul(ps_z[u % 2][:, k, :], left[:, u, k * P:(k + 1) * P],
                                                  right[:, u, k // TG, :], start=True, stop=True)
                        mm.then_inc(z_mm, 1)
                    if live(turn, u, -2):
                        v = (u - 2) % SL
                        m = turn * SL + u - 2 + l * QUADS
                        pe.wait_ge(msg_ready, m + 1)
                        if live(turn, u, -4):
                            pe.wait_ge(acc_done, GQ * (m - 1))
                        sums = ps_s[v % 2][:, 0:GQ * 2 * W].rearrange("p (g s w) -> p g s w", g=GQ, s=2)
                        bits = hot[:, v, :, :].bitcast(BF16).rearrange("p t (w two) -> p t w two", two=2)
                        for g in range(GQ):
                            for k in range(TG):
                                mm = nc.tensor.matmul(sums[:, g, 0, :], msg[:, v % 2, g * TG + k, :],
                                                      hot[:, v, g * TG + k, :], start=k == 0, stop=k == TG - 1)
                            if l == 0:
                                for k in range(TG):
                                    mm = nc.tensor.matmul(sums[:, g, 1, :], ones_bf[:], bits[:, g * TG + k, :, 1],
                                                          start=k == 0, stop=k == TG - 1)
                        mm.then_inc(sums_mm, 1)

                def fast():
                    steps(pe, products, 0, 2)

                def general():
                    def tile(t):
                        m = t + l * TILES
                        pe.wait_ge(g_edge_in, 16 * (m + 1))
                        if l or not isinstance(t, int):
                            pe.wait_ge(g_zb, m)
                        nc.tensor.matmul(ps_z[0][:, 0, :], left[W:P, 0, 0:P], right[W:P, 0, 0, :],
                                         start=True, stop=True).then_inc(g_z_mm, 1)
                        with pe.Fori(0, CH) as w:
                            pe.wait_ge(g_msg, m + 1)
                            pe.wait_ge(g_hot, m * CH + w + 1)
                            bits = hot_w[:].bitcast(BF16).rearrange("p (w two) -> p w two", two=2)
                            mm = nc.tensor.matmul(ps_s[0][:, 0:P], msg[:, 0, 0, :], hot_w[:],
                                                  start=True, stop=True)
                            if l == 0:
                                mm = nc.tensor.matmul(ps_s[0][:, P:2 * P], ones_bf[:], bits[:, :, 1],
                                                      start=True, stop=True)
                            mm.then_inc(g_sums, 1)

                    first_then_rest(pe, tile, TILES)

                pe.wait_ge(right_ready, l + 1)
                if l == 0:
                    pe.wait_ge(flag_ready, 1)
                choose(pe, fast, general)

                pe.wait_ge(edges_done, l + 1)
                if l == 0:
                    for c in range(CH):
                        mm = nc.tensor.matmul(ps_n[:, c:c + 1], acc[:, 1, c * P:(c + 1) * P], ident[:, 0:1],
                                              start=True, stop=True)
                    mm.then_inc(cnt_cols, 1)
                    pe.wait_ge(inv_ready, 1)
                for g in range(2):
                    spread(l, g)

            for g in range(NG):
                if g + 2 < NG:
                    spread(1, g + 2)
                pe.wait_ge(h_t_ready, 2 * NG + g + 1)
                if g >= TP:
                    pe.wait_ge(out_ready, g - TP + 1)
                transpose(g, lambda c: h_t[:, c * P:(c + 1) * P])

        @block.scalar
        def _(act):
            act.wait_ge(var_ready, 1)
            nc.scalar.activation(rstd[:], var[:], ACT.Sqrt).then_inc(root_ready, 1)
            act.wait_ge(var_ready, 2)
            nc.scalar.activation(bn_tmp[:, :, 1], bn_tmp[:, :, 0], ACT.Sqrt).then_inc(root_ready, 1)
            act.preload_act_table_set(LOG_EXP)
            act.wait_ge(shift_ready, 1)
            for g in range(DVE_GROUPS, NG):
                for c in group(g)[0]:
                    a = nc.scalar.activation(h_rows[:, c, :], x_rows[:, c, :], ACT.Relu,
                                             bias=shift[:, c:c + 1], scale=rstd[:, c:c + 1])
                a.then_inc(h_ready_act, 1)
            for l in range(2):
                def b_table_rows(i):
                    for u in range(TP):
                        act.wait_ge(tab_mm, l * 2 * CH + i * TP + u + 1)
                        if l or not isinstance(i, int):
                            act.wait_ge(b_out[u], 16 * (i + l * TURN_N))
                        nc.scalar.copy(tab[:, 1, u, :], bank[u][:, 0:Z]).then_inc(b_rows, 1)

                first_then_rest(act, b_table_rows, TURN_N)

                def logs(turn, u):
                    if not live(turn, u):
                        return
                    h = u % 2
                    m = turn * SL + u + l * QUADS
                    act.wait_ge(z_ready, m + 1)
                    if live(turn, u, -2):
                        act.wait_ge(soft_ready, m - 1)
                    nc.scalar.activation(lnz[:, h], z[:, h], ACT.Exp).then_inc(exp_ready, 1)
                    act.wait_ge(exp_ready, m + 1)
                    nc.scalar.activation(lnz[:, h], lnz[:, h], ACT.Ln, bias=1.0).then_inc(ln_ready, 1)
                    act.wait_ge(ln_ready, m + 1)
                    if live(turn, u, -2):
                        act.wait_ge(msg_ready, m - 1)
                    nc.scalar.activation(gate[:, h], lnz[:, h, :, 0:F], ACT.Exp, scale=-1.0).then_inc(gate_ready, 1)

                def fast():
                    steps(act, logs, 0, 0)

                def general():
                    def tile(t):
                        m = t + l * TILES
                        act.wait_ge(g_z, m + 1)
                        nc.scalar.activation(lnz[:, 0, 0], z[:, 0, 0], ACT.Exp).then_inc(g_exp, 1)
                        act.wait_ge(g_exp, m + 1)
                        nc.scalar.activation(lnz[:, 0, 0], lnz[:, 0, 0], ACT.Ln, bias=1.0).then_inc(g_ln, 1)
                        act.wait_ge(g_ln, m + 1)
                        nc.scalar.activation(gate[:, 0, 0], lnz[:, 0, 0, 0:F], ACT.Exp, scale=-1.0)\
                            .then_inc(g_gate, 1)

                    first_then_rest(act, tile, TILES)

                if l == 0:
                    act.wait_ge(flag_ready, 1)
                choose(act, fast, general)

        @block.vector
        def _(dve):
            done = [0]

            def link(ins):
                done[0] += 1
                ins.then_inc(prep, 1)
                dve.wait_ge(prep, done[0])

            for g in range(NG):
                dve.wait_ge(x_in[g], 16)
                for c in group(g)[0]:
                    st = nc.vector.bn_stats(stats[:, c, :], x_rows[:, c, :])
            link(st)
            mean_e, mean_o, m2_e, m2_o = stats[:, :, 1], stats[:, :, 4], stats[:, :, 2], stats[:, :, 5]
            nc.vector.tensor_tensor(mean[:], mean_e, mean_o, ALU.add)
            nc.vector.tensor_tensor(tmp[:], mean_e, mean_o, ALU.subtract)
            link(nc.vector.tensor_tensor(var[:], m2_e, m2_o, ALU.add))
            nc.vector.tensor_scalar(mean[:], mean[:], 0.5, None, ALU.mult)
            link(nc.vector.tensor_tensor(tmp[:], tmp[:], tmp[:], ALU.mult))
            link(nc.vector.scalar_tensor_tensor(var[:], tmp[:], F / 4.0, var[:], ALU.mult, ALU.add))
            nc.vector.tensor_scalar(var[:], var[:], 1.0 / F, LN_EPS, ALU.mult, ALU.add).then_inc(var_ready, 1)
            dve.wait_ge(w_in, W_LOADS)
            nc.vector.tensor_scalar(bn_tmp[:, :, 0], bn[:, :, 3], BN_EPS, None, ALU.add).then_inc(var_ready, 1)
            dve.wait_ge(root_ready, 1)
            link(nc.vector.reciprocal(rstd[:], rstd[:]))
            nc.vector.scalar_tensor_tensor(shift[:], mean[:], -1.0, rstd[:], ALU.mult, ALU.mult)\
                .then_inc(shift_ready, 1)
            for g in range(DVE_GROUPS):
                for c in group(g)[0]:
                    nrm = nc.vector.tensor_scalar(h_rows[:, c, :], x_rows[:, c, :], mean[:, c:c + 1],
                                                  rstd[:, c:c + 1], ALU.subtract, ALU.mult)
                nrm.then_inc(h_ready, 1)

            nc.vector.tensor_scalar(w_node[:, :, :, 0, :], w_node[:, :, :, 0, :], -1.0, None, ALU.mult)
            nc.vector.tensor_scalar(w_edge[W:P, :, 0, :], w_edge[W:P, :, 0, :], -1.0, None, ALU.mult)
            nc.vector.tensor_scalar(bias[:, :, 0, :], bias[:, :, 0, :], -1.0, None, ALU.mult).then_inc(w_ready, 1)

            for g in range(NG):
                dve.wait_ge(turned, g + 1)
                cols = group(g)[1]
                nc.vector.tensor_scalar(h_t[:, cols], bank[g % TP][:, 0:cols.stop - cols.start],
                                        0.0, None, ALU.max).then_inc(h_t_ready, 1)

            dve.wait_ge(root_ready, 2)
            link(nc.vector.reciprocal(bn_tmp[:, :, 1], bn_tmp[:, :, 1]))
            link(nc.vector.tensor_tensor(bn_scale[:], bn[:, :, 0], bn_tmp[:, :, 1], ALU.mult))
            link(nc.vector.tensor_tensor(bn_tmp[:, :, 0], bn[:, :, 2], bn_scale[:], ALU.mult))
            link(nc.vector.tensor_tensor(bn_shift[:], bn[:, :, 1], bn_tmp[:, :, 0], ALU.subtract))

            dve.wait_ge(idx_in, IDX_LOADS)
            dve.wait_ge(iota_ready, 4)
            nc.vector.tensor_copy(iota_f[:], iota_i[:])
            nc.vector.tensor_copy(part_f[:], part_i[:])
            nc.vector.tensor_copy(first_f[:], first_i[:])
            link(nc.vector.tensor_copy(dst_f[:], dst_i[:, 0:TILES]))
            nc.vector.tensor_scalar(target[:], first_f[0:W, :], part_f[0:W, :], None, ALU.add)
            link(nc.vector.tensor_tensor(rel[:].rearrange("p (g t) -> p g t", t=TG),
                                         dst_f[:].rearrange("p (g t) -> p g t", t=TG),
                                         first_f[:].unsqueeze(2).to_broadcast((P, GROUPS, TG)), ALU.subtract))
            link(nc.vector.tensor_scalar(outside[:], rel[:], 0.0, None, ALU.is_lt))
            link(nc.vector.scalar_tensor_tensor(outside2[:], rel[:], W - 1.0, outside[:], ALU.is_gt, ALU.max))
            if FORCE_GENERAL:
                link(nc.vector.memset(outside2[:], 1.0))
            nc.vector.tensor_reduce(worst[:], outside2[:], AX.X, ALU.max).then_inc(worst_ready, 1)

            dve.wait_ge(worst_spread, 1)
            nc.vector.tensor_copy(flag[:], worst_all[:]).then_inc(flag_ready, 1)

            for l in range(2):
                for j in range(SL):
                    mv = nc.vector.tensor_copy(
                        right[W:P, j], w_edge[W:P, l].rearrange("p j f -> p (j f)").unsqueeze(1)
                        .to_broadcast((FE, GQ, Z)))
                mv.then_inc(right_ready, 1)

                def a_table_rows(i):
                    for u in range(TP):
                        dve.wait_ge(tab_mm, l * 2 * CH + CH + i * TP + u + 1)
                        if l or not isinstance(i, int):
                            dve.wait_ge(a_out[u], 16 * (i + l * TURN_N))
                        nc.vector.tensor_tensor(tab[:, 0, u, :], bank[u][:, 0:Z],
                                                bias[:, l].rearrange("p j f -> p (j f)"),
                                                ALU.add).then_inc(a_rows, 1)

                first_then_rest(dve, a_table_rows, TURN_N)
                dve.wait_ge(acc_zero, l + 1)

                def elementwise(turn, u):
                    if live(turn, u):
                        h = u % 2
                        m = turn * SL + u + l * QUADS
                        dve.wait_ge(z_mm, m + 1)
                        dve.wait_ge(gath_in[u], 16 * TQ * (turn + l * used(u) + 1))
                        if live(turn, u, -2):
                            dve.wait_ge(soft_ready, m - 1)
                        nc.vector.tensor_tensor(z[:, h], ps_z[h][:], gath[:, u], ALU.add).then_inc(z_ready, 1)
                    if live(turn, u, -2):
                        rows = [first_row(dve, (turn * SL + u - 2) * GQ + g) for g in range(GQ)]
                    if live(turn, u, -1):
                        h = (u - 1) % 2
                        m = turn * SL + u - 1 + l * QUADS
                        dve.wait_ge(ln_ready, m + 1)
                        if live(turn, u, -3):
                            dve.wait_ge(msg_ready, m - 1)
                        nc.vector.scalar_tensor_tensor(soft[:, h], lnz[:, h, :, F:Z], CAP, z[:, h, :, F:Z],
                                                       ALU.min, ALU.max).then_inc(soft_ready, 1)
                    if live(turn, u, -1):
                        h = (u - 1) % 2
                        m = turn * SL + u - 1 + l * QUADS
                        dve.wait_ge(gate_ready, m + 1)
                        dve.wait_ge(soft_ready, m + 1)
                        if live(turn, u, -3):
                            dve.wait_ge(sums_mm, m - 1)
                        nc.vector.tensor_tensor(msg[:, h], gate[:, h], soft[:, h],
                                                ALU.mult).then_inc(msg_ready, 1)
                    for g in range(GQ):
                        if live(turn, u, -2):
                            h = u % 2
                            m = turn * SL + u - 2 + l * QUADS
                            if g == 0:
                                dve.wait_ge(sums_mm, m + 1)
                            if live(turn, u, -3) or g:
                                dve.wait_ge(acc_done, GQ * m + g)
                            sums = ps_s[h][:, 0:GQ * 2 * W].rearrange("p (g s w) -> p g s w", g=GQ, s=2)
                            k = 2 - l
                            there = acc[:, 0:k, bass.ds(rows[g], W)]
                            nc.vector.tensor_tensor(there, there, sums[:, g, 0:k, :], ALU.add).then_inc(acc_done, 1)
                        if live(turn, u, 2):
                            t2, v = at(turn, u, 2)
                            n = t2 * SL + v
                            m = n + l * QUADS
                            if g == 0:
                                dve.wait_ge(dst_in[v], 16 * (t2 + l * used(v) + 1))
                                if live(t2, v, -SL):
                                    dve.wait_ge(z_mm, m - SL + 1)
                                    dve.wait_ge(sums_mm, m - SL + 1)
                            part = slice(g * TG * P, (g + 1) * TG * P)
                            nc.vector.tensor_scalar(left[0:W, v, part], dst_b[:, v, part],
                                                    target[:, bass.ds(n * GQ + g, 1)], None, ALU.is_equal)
                            if g == GQ - 1:
                                nc.vector.tensor_tensor(
                                    hot[:, v], iota_f[:, 0:W].unsqueeze(1).to_broadcast((P, TQ, W)),
                                    rel[:, bass.ds(n * TQ, TQ)].unsqueeze(2).to_broadcast((P, TQ, W)),
                                    ALU.is_equal).then_inc(hots_ready, 1)

                def fast():
                    steps(dve, elementwise, 2, 2)
                    dve.wait_ge(acc_done, GQ * QUADS * (l + 1))
                    dve.sem_inc(edges_done, 1)

                def general():
                    def tile(t):
                        m = t + l * TILES
                        dve.wait_ge(g_z_mm, m + 1)
                        dve.wait_ge(g_rows_in, 32 * (m + 1))
                        nc.vector.tensor_tensor(z[:, 0, 0], ps_z[0][:, 0], gath[:, 0, 0], ALU.add).then_inc(g_zb, 1)
                        dve.wait_ge(g_zb, m + 1)
                        nc.vector.tensor_tensor(z[:, 0, 0], z[:, 0, 0], gath[:, 0, 1], ALU.add).then_inc(g_z, 1)
                        dve.wait_ge(g_ln, m + 1)
                        nc.vector.scalar_tensor_tensor(soft[:, 0, 0], lnz[:, 0, 0, F:Z], CAP, z[:, 0, 0, F:Z],
                                                       ALU.min, ALU.max).then_inc(g_soft, 1)
                        nc.vector.tensor_copy(rel_w[:], dst_f[:, bass.ds(t, 1)]).then_inc(g_rel, 1)
                        dve.wait_ge(g_gate, m + 1)
                        dve.wait_ge(g_soft, m + 1)
                        if l or not isinstance(t, int):
                            dve.wait_ge(g_acc, m * CH)
                        nc.vector.tensor_tensor(msg[:, 0, 0], gate[:, 0, 0], soft[:, 0, 0],
                                                ALU.mult).then_inc(g_msg, 1)
                        with dve.Fori(0, CH) as w:
                            dve.wait_ge(g_rel, m * (CH + 1) + w + 1)
                            nc.vector.tensor_scalar(hot_w[:], iota_f[:], rel_w[:], None, ALU.is_equal)\
                                .then_inc(g_hot, 1)
                            dve.wait_ge(g_hot, m * CH + w + 1)
                            nc.vector.tensor_scalar(rel_w[:], rel_w[:], -float(P), None, ALU.add).then_inc(g_rel, 1)
                            dve.wait_ge(g_sums, m * CH + w + 1)
                            k = 2 - l
                            there = acc[:, 0:k, bass.ds(w * P, P)]
                            nc.vector.tensor_tensor(
                                there, there, ps_s[0][:, 0:k * P].rearrange("p (s w) -> p s w", s=k),
                                ALU.add).then_inc(g_acc, 1)

                    first_then_rest(dve, tile, TILES)
                    dve.wait_ge(g_acc, CH * TILES * (l + 1))
                    dve.sem_inc(edges_done, 1)

                if l == 0:
                    dve.wait_ge(flag_ready, 1)
                choose(dve, fast, general)

                if l == 0:
                    dve.wait_ge(cnt_cols, 1)
                    link(nc.vector.tensor_scalar(inv_cnt[:], ps_n[:, 0:CH], 1.0, None, ALU.max))
                    nc.vector.reciprocal(inv_cnt[:], inv_cnt[:]).then_inc(inv_ready, 1)

                def mean_of(g):
                    cols = group(g)[1]
                    dve.wait_ge(inv_spread, l * NG + g + 1)
                    nc.vector.scalar_tensor_tensor(mean_t[:, cols], acc[:, 0, cols], bn_scale[:, l:l + 1],
                                                   ps_s[g % 2][:, 0:cols.stop - cols.start],
                                                   ALU.mult, ALU.mult).then_inc(mean_ready, 1)

                mean_of(0)
                for g in range(NG):
                    if g + 1 < NG:
                        mean_of(g + 1)
                    cols = group(g)[1]
                    dve.wait_ge(mean_ready, l * NG + g + 1)
                    nc.vector.scalar_tensor_tensor(h_t[:, cols], mean_t[:, cols], bn_shift[:, l:l + 1], h_t[:, cols],
                                                   ALU.add, ALU.add).then_inc(h_t_ready, 1)

            for g in range(NG):
                dve.wait_ge(turned, NG + g + 1)
                chunks = group(g)[0]
                nc.vector.tensor_tensor(h_rows[:, chunks.start:chunks.stop], x_rows[:, chunks.start:chunks.stop],
                                        bank[g % TP][:, 0:len(chunks) * P].rearrange("p (c f) -> p c f", f=F),
                                        ALU.add).then_inc(out_ready, 1)


_WEIGHTS = [f"{n}{l}" for l in (1, 2) for n in ("Wf", "bf", "Ws", "bs", "gamma", "beta", "rmean", "rvar")]


def kernel(**inputs):
    import concourse.bacc as bacc
    from concourse.bass_utils import run_bass_kernel_spmd

    x = np.zeros((NP, F), np.float32)
    x[:N_NODES] = np.asarray(inputs["x"])
    src = np.zeros((EP,), np.int32)
    src[:N_EDGES] = np.asarray(inputs["src"])
    dst = np.full((EP,), N_NODES, np.int32)
    dst[:N_EDGES] = np.asarray(inputs["dst"])
    edge = np.zeros((EP, FE), np.float32)
    edge[:N_EDGES] = np.asarray(inputs["edge_attr_64"])
    cols = np.zeros((2, P, TILES + 1), np.int32)
    cols[0, :, :TILES] = src.reshape(TILES, P).T
    cols[1, :, :TILES] = dst.reshape(TILES, P).T
    arrays = {
        "x": x,
        "src_cols": cols[0],
        "dst_cols": cols[1],
        "dst_row": dst,
        "dst_first": np.ascontiguousarray(dst[::TG * P]),
        "edge_t": np.ascontiguousarray(edge.T),
    }
    w = {n: np.asarray(inputs[f"L0_gnn_{n}"]) for n in _WEIGHTS}
    both = [np.concatenate([w[f"Wf{l}"], w[f"Ws{l}"]], axis=1) for l in (1, 2)]
    arrays["w_node_in"] = np.ascontiguousarray(
        np.concatenate([b[a:a + F] for b in both for a in (0, F)], axis=1))
    arrays["w_edge_in"] = np.ascontiguousarray(np.concatenate([b[2 * F:] for b in both], axis=1))
    arrays["bias_in"] = np.concatenate([w[f"{n}{l}"] for l in (1, 2) for n in ("bf", "bs")])
    arrays["bn_in"] = np.ascontiguousarray(
        np.stack([w[f"{n}{l}"] for l in (1, 2) for n in ("gamma", "beta", "rmean", "rvar")], axis=1))

    nc = bacc.Bacc("TRN2", target_bir_lowering=False, num_devices=1)
    aps = {n: nc.dram_tensor(f"in_{n}", a.shape, mybir.dt.from_np(a.dtype), kind="ExternalInput").ap()
           for n, a in arrays.items()}
    out = nc.dram_tensor("out", (N_NODES, F), F32, kind="ExternalOutput").ap()
    build(nc, out=out, **aps)
    r = run_bass_kernel_spmd(nc, [{f"in_{n}": a for n, a in arrays.items()}], core_ids=[0])
    return r.results[0]["out"]
```

```python
from contextlib import ExitStack

import numpy as np

import concourse.bass as bass
from concourse import mybir

P = 128
F = 128
FE = 64
Z = 2 * F
N_NODES = 3125
CH = -(-N_NODES // P)
NP = CH * P
N_EDGES = 50000
TQ = 4
QE = TQ * P
QUADS = -(-N_EDGES // QE)
FULL = -(-N_EDGES // P)
EP = QUADS * QE
TILES = EP // P
GQ = 2
TG = TQ // GQ
GROUPS = QUADS * GQ
W = 64
SL = 6
ES = 3
IDX_SETS = -(-QUADS // ES)
COLS = IDX_SETS * ES * TQ
LOG_EXP = "natural_log_exp_and_others"
NG = -(-CH // 4)
TP = 5
TURN_N = CH // TP
SQ = 32
LAST = N_NODES // P
BNS = 6
LN_EPS = 1e-5
BN_EPS = 1e-5
CAP = 40.0

ALU = mybir.AluOpType
ACT = mybir.ActivationFunctionType
F32 = mybir.dt.float32
BF16 = mybir.dt.bfloat16
I32 = mybir.dt.int32
AX = mybir.AxisListType
RMAX = bass.bass_isa.ReduceOp.max


def group(g):
    a, b = 4 * g, min(4 * g + 4, CH)
    return range(a, b), slice(a * P, b * P)


def build(nc, x, src_cols, dst_cols, dst_row, dst_first, edge_t, w_node_in, w_edge_in, bias_in, bn_in, out):
    ctx = ExitStack()
    with ctx:
        def sb(name, shape, dt=F32):
            return ctx.enter_context(nc.sbuf_tensor(name, shape, dt))

        def ps(name, shape, dt=F32):
            return ctx.enter_context(nc.psum_tensor(name, shape, dt))

        def sem(name):
            return ctx.enter_context(nc.semaphore(name))

        a_table = nc.dram_tensor("a_table", (NP, Z), F32).ap()
        b_table = nc.dram_tensor("b_table", (NP, Z), F32).ap()

        x_rows = sb("x_rows", [P, CH, F])
        acc = sb("acc", [P, 2, NP])
        node = sb("node", [P, CH * 2 * Z])
        h_rows = node[:, 0:CH * F].rearrange("p (c f) -> p c f", f=F)
        h_t = node[:, CH * 2 * Z - NP:CH * 2 * Z]
        ahead = node[:].rearrange("p (c s z) -> p c s z", s=2, z=Z)
        edges_col = sb("edges_col", [P, CH])
        inv = sb("inv", [P, CH])
        stats = sb("stats", [P, CH, BNS])
        shift = sb("shift", [P, CH])
        tmp = sb("tmp", [P, CH])
        mean = sb("mean", [P, CH])
        var = sb("var", [P, CH])
        rstd = sb("rstd", [P, CH])
        ident = sb("ident", [P, P])
        ones_bf = sb("ones_bf", [P, P], BF16)
        w_node = sb("w_node", [P, 2, 2, 2, F])
        w_edge = sb("w_edge", [P, 2, 2, F])
        bias = sb("bias", [P, 2, 2, F])
        bn = sb("bn", [P, 2, 4])
        bn_scale = sb("bn_scale", [P, 2])
        bn_shift = sb("bn_shift", [P, 2])
        bn_tmp = sb("bn_tmp", [P, 2, 2])
        h_part = sb("h_part", [P, 2, P])
        shift_sum = sb("shift_sum", [P, 1])
        scales = sb("scales", [P, 2, P])
        ones_row = sb("ones_row", [1, P])

        src_i = sb("src_i", [P, COLS], I32)
        dst_i = sb("dst_i", [P, COLS], I32)
        first_i = sb("first_i", [P, GROUPS], I32)
        first_f = sb("first_f", [P, GROUPS])
        dst_f = sb("dst_f", [P, TILES])
        rel = sb("rel", [P, TILES])
        outside = sb("outside", [P, TILES])
        outside2 = sb("outside2", [P, TILES])
        worst = sb("worst", [P, 1])
        worst_all = sb("worst_all", [P, 1])
        flag = sb("flag", [P, 1], I32)
        target = sb("target", [W, GROUPS])
        iota_i = sb("iota_i", [P, P], I32)
        iota_f = sb("iota_f", [P, P])
        part_i = sb("part_i", [P, 1], I32)
        part_f = sb("part_f", [P, 1])

        left = sb("left", [P, ES, QE])
        right = sb("right", [P, ES, GQ, Z])
        dst_b = sb("dst_b", [W, ES, QE], I32)
        idx = sb("idx", [P, 2, ES * TQ], I32)
        hot = sb("hot", [P, SL, TQ, W])

        work = sb("work", [P, 2, CH * Z])
        b_stage = work[:, 0, :].rearrange("p (c z) -> p c z", z=Z)
        a_stage = work[:, 1, :].rearrange("p (c z) -> p c z", z=Z)

        def cut(half, start, s, t, n):
            return work[:, half, start:start + s * t * n].rearrange("p (s t n) -> p s t n", s=s, t=t)

        gath = cut(0, 0, SL, TQ, Z)
        squares = work[:, 0, 0:CH * SQ].rearrange("p (c q) -> p c q", q=SQ)
        z = cut(1, 0, 2, TQ, Z)
        lnz = cut(1, 2 * TQ * Z, 2, TQ, Z)
        soft = cut(1, 4 * TQ * Z, 2, TQ, F)
        gate = cut(1, 5 * TQ * Z, 2, TQ, F)
        msg = sb("msg", [P, 2, TQ, F])
        rel_w = sb("rel_w", [P, 1])
        hot_w = sb("hot_w", [P, P])

        ps_z = [ps(f"ps_z{i}", [P, TQ, Z]) for i in range(2)]
        ps_s = [ps(f"ps_s{i}", [P, 512]) for i in range(2)]
        ps_n = ps("ps_n", [P, 512])
        ps_t = ps("ps_t", [P, 512])
        turn_bank = [ps_s[0], ps_s[1], ps_t]
        ahead_bank = [ps_n, ps_t]
        bank = [ps_z[i][:, 2 * j:2 * j + 2, :].rearrange("p t z -> p (t z)") for i in range(2) for j in range(2)]
        bank.append(ps_n[:, :])

        x_in = [sem(f"x_in{g}") for g in range(NG)]
        idx_in = sem("idx_in")
        w_in = sem("w_in")
        iota_ready = sem("iota_ready")
        ident_ready = sem("ident_ready")
        acc_zero = sem("acc_zero")
        prep = sem("prep")
        var_ready = sem("var_ready")
        root_ready = sem("root_ready")
        shift_ready = sem("shift_ready")
        h_ready = sem("h_ready")
        h_ready_act = sem("h_ready_act")
        turned = sem("turned")
        h_t_ready = sem("h_t_ready")
        h_t_ready_act = sem("h_t_ready_act")
        w_ready = sem("w_ready")
        worst_ready = sem("worst_ready")
        worst_spread = sem("worst_spread")
        flag_ready = sem("flag_ready")
        right_ready = sem("right_ready")
        tab_mm = sem("tab_mm")
        a_rows = sem("a_rows")
        b_rows = sem("b_rows")
        a_out = sem("a_out")
        b_out = sem("b_out")
        bn_ready = sem("bn_ready")
        base_ready = sem("base_ready")
        spread_mm = sem("spread_mm")
        h_part_ready = sem("h_part_ready")
        w_scaled = sem("w_scaled")
        ahead_mm = sem("ahead_mm")
        ahead_rows = sem("ahead_rows")
        inv_ready = sem("inv_ready")
        fold_mm = sem("fold_mm")
        edge_in = [sem(f"edge_in{i}") for i in range(ES)]
        dst_in = [sem(f"dst_in{i}") for i in range(ES)]
        win_in = [sem(f"win_in{i}") for i in range(ES)]
        idx_set = sem("idx_set")
        gath_in = [sem(f"gath_in{i}") for i in range(SL)]
        hots_ready = sem("hots_ready")
        z_mm = sem("z_mm")
        z_ready = sem("z_ready")
        exp_ready = sem("exp_ready")
        ln_ready = sem("ln_ready")
        soft_ready = sem("soft_ready")
        gate_ready = sem("gate_ready")
        msg_ready = sem("msg_ready")
        sums_mm = sem("sums_mm")
        acc_done = sem("acc_done")
        g_edge_in = sem("g_edge_in")
        g_rows_in = sem("g_rows_in")
        g_idx_set = sem("g_idx_set")
        g_z_mm = sem("g_z_mm")
        g_zb = sem("g_zb")
        g_z = sem("g_z")
        g_exp = sem("g_exp")
        g_ln = sem("g_ln")
        g_soft = sem("g_soft")
        g_gate = sem("g_gate")
        g_msg = sem("g_msg")
        g_rel = sem("g_rel")
        g_hot = sem("g_hot")
        g_sums = sem("g_sums")
        g_acc = sem("g_acc")
        edges_done = sem("edges_done")
        out_ready = sem("out_ready")
        out_sent = sem("out_sent")

        STORES = [(a, a + TP) for a in range(0, CH - TP, TP)] + [(CH - TP, CH - 2), (CH - 2, CH)]
        IDX_LOADS, W_LOADS = 3 * 16, 4 * 16
        ACT_GROUPS = 3
        DVE_GROUPS = NG - ACT_GROUPS
        TURNS = QUADS // SL
        REST = QUADS % SL

        def used(u):
            return TURNS + (1 if u < REST else 0)

        def gathered(l, turn, u):
            last = isinstance(turn, int) and SL * turn + u == QUADS - 1
            passed = l if u == (QUADS - 1) % SL else 0
            return 16 * (TQ * (turn + 1 + l * used(u)) - (TILES - FULL) * (last + passed))

        def loads(l, turn, u, each=1):
            return 16 * each * (turn * (SL // ES) + u // ES + 1 + l * (QUADS // ES + (u % ES < QUADS % ES)))

        def steps(eng, step, ahead, behind):
            lo = 1
            hi = TURNS - 1
            for n in range(-ahead, lo * SL):
                step(n // SL, n % SL)
            with eng.Fori(0, hi - lo) as i:
                for u in range(SL):
                    step(i + lo, u)
            for n in range(hi * SL, QUADS + behind):
                step(n // SL, n % SL)

        def first_then_rest(eng, body, n):
            body(0)
            with eng.Fori(1, n) as i:
                body(i)

        AHEAD = CH - TURNS

        def ahead_chunk(turn, u, when):
            if u != when or isinstance(turn, int) and not 0 <= turn < TURNS:
                return None
            return turn + AHEAD

        def live(turn, u, shift=0):
            return not isinstance(turn, int) or 0 <= SL * turn + u + shift < QUADS

        def at(turn, u, shift):
            m = u + shift
            return (turn + m // SL if m // SL else turn), m % SL

        def first_row(eng, g):
            return eng.value_load(first_i[0:1, bass.ds(g, 1)], min_val=0, max_val=NP - W)

        def targets(eng, turn, u):
            eng.dma_start(dst_b[:, u % ES, :], dst_row[None, bass.ds((turn * SL + u) * QE, QE)].to_broadcast((W, QE)))\
                .then_inc(dst_in[u % ES], 16)

        def choose(eng, fast, general):
            f = eng.value_load(flag[0:1, 0:1], min_val=0, max_val=1)
            with eng.If(f == 0):
                fast()
            with eng.Else():
                general()

        block = ctx.enter_context(nc.Block())

        @block.sync
        def _(sp):
            for g in range(NG):
                chunks, cols = group(g)
                sp.dma_start(x_rows[:, chunks.start:chunks.stop, :],
                             x[cols, :].rearrange("(c p) f -> p c f", p=P)).then_inc(x_in[g], 16)
            sp.dma_start(w_node[:].rearrange("p l s j f -> p (l s j f)"), w_node_in).then_inc(w_in, 16)
            sp.dma_start(w_edge[P - FE:P].rearrange("p l j f -> p (l j f)"), w_edge_in).then_inc(w_in, 16)
            sp.dma_start(bias[:].rearrange("p l j f -> p (l j f)"),
                         bias_in[None, :].to_broadcast((P, 2 * Z))).then_inc(w_in, 16)
            sp.dma_start(bn[:].rearrange("p l k -> p (l k)"), bn_in).then_inc(w_in, 16)
            sp.dma_start(dst_i[:], dst_cols).then_inc(idx_in, 16)
            sp.dma_start(first_i[:], dst_first[None, :].to_broadcast((P, GROUPS))).then_inc(idx_in, 16)
            sp.dma_start(src_i[:], src_cols).then_inc(idx_in, 16)

            def edges(turn, u):
                sp.dma_start(left[W:P, u % ES, :], edge_t[:, bass.ds((turn * SL + u) * QE, QE)])\
                    .then_inc(edge_in[u % ES], 16)

            def first_edges():
                for u in range(ES):
                    targets(sp, 0, u)
                    edges(0, u)

            def nothing():
                pass

            first_edges()

            for l in range(2):
                def load(turn, u):
                    if not live(turn, u):
                        return
                    n = turn * SL + u
                    if live(turn, u, -ES):
                        sp.wait_ge(z_mm, n + l * QUADS - ES + 1)
                        edges(turn, u)
                    rows = [first_row(sp, n * GQ + k) for k in range(GQ)]
                    if not live(turn, u, -1):
                        sp.wait_ge(a_out, 16 * (l + 1) * len(STORES))
                    for k in range(GQ):
                        sp.dma_start(right[0:W, u % ES, k, :], a_table[bass.ds(rows[k], W), :])\
                            .then_inc(win_in[u % ES], 16)

                def first_edges_again():
                    sp.wait_ge(z_mm, QUADS)
                    first_edges()

                def store(table, rows_ready, stage, sent):
                    for a, b in STORES:
                        sp.wait_ge(rows_ready, l * CH + b)
                        sp.dma_start(table[a * P:b * P, :].rearrange("(c p) z -> p c z", p=P),
                                     stage[:, a:b, :]).then_inc(sent, 16)

                if l:
                    choose(sp, first_edges_again, nothing)
                store(b_table, b_rows, ahead[:, :, 1, :] if l else b_stage, b_out)
                store(a_table, a_rows, ahead[:, :, 0, :] if l else a_stage, a_out)

                def fast():
                    steps(sp, load, 0, 0)

                def general():
                    if l == 0:
                        sp.wait_ge(edge_in[0], 16)

                    def tile(t):
                        if l or not isinstance(t, int):
                            sp.wait_ge(g_z_mm, t + l * TILES)
                        sp.dma_start(left[W:P, 0, 0:P], edge_t[:, bass.ds(t * P, P)]).then_inc(g_edge_in, 16)

                    first_then_rest(sp, tile, TILES)

                if l == 0:
                    sp.wait_ge(idx_in, IDX_LOADS)
                    sp.wait_ge(flag_ready, 1)
                choose(sp, fast, general)

            for g in range(NG):
                chunks, cols = group(g)
                whole = min(chunks.stop, LAST) - chunks.start
                sp.wait_ge(out_ready, NG + g + 1)
                if whole:
                    sp.dma_start(out[cols.start:cols.start + whole * P, :].rearrange("(c p) f -> p c f", p=P),
                                 x_rows[:, chunks.start:chunks.start + whole, :]).then_inc(out_sent, 16)
            sp.dma_start(out[LAST * P:N_NODES, :], x_rows[0:N_NODES - LAST * P, LAST, :]).then_inc(out_sent, 16)
            sp.wait_ge(out_sent, 16 * (-(-LAST // 4) + 1))

        @block.gpsimd
        def _(pool):
            nc.gpsimd.memset(ident[:], 0.0).then_inc(iota_ready, 1)
            nc.gpsimd.iota(iota_i[:], pattern=[[1, P]], base=0, channel_multiplier=0).then_inc(iota_ready, 1)
            nc.gpsimd.iota(part_i[:], pattern=[[0, 1]], base=0, channel_multiplier=1).then_inc(iota_ready, 1)
            nc.gpsimd.memset(ones_bf[:], 1.0).then_inc(iota_ready, 1)
            nc.gpsimd.memset(ones_row[:], 1.0).then_inc(iota_ready, 1)
            pool.wait_ge(iota_ready, 5)
            nc.gpsimd.affine_select(out=ident[:], in_=ident[:], compare_op=ALU.not_equal, fill=1.0, base=0,
                                    pattern=[[-1, P]], channel_multiplier=1).then_inc(ident_ready, 1)
            nc.gpsimd.memset(acc[:], 0.0).then_inc(acc_zero, 1)
            pool.wait_ge(w_in, W_LOADS)
            for k, gate_columns in enumerate((w_node[:, :, :, 0, :], w_edge[W:P, :, 0, :], bias[:, :, 0, :])):
                nc.gpsimd.tensor_scalar(gate_columns, gate_columns, -1.0, None, ALU.mult).then_inc(w_ready, 1)
                pool.wait_ge(w_ready, k + 1)
            pool.wait_ge(worst_ready, 1)
            nc.gpsimd.partition_all_reduce(worst_all[:], worst[:], P, RMAX).then_inc(worst_spread, 1)
            pool.wait_ge(idx_in, IDX_LOADS)
            for l in range(2):
                pool.wait_ge(b_out, 16 * (l + 1) * len(STORES))

                def gather(turn, u):
                    if u % ES == ES - 1 and live(turn, u, 1):
                        t2, v = at(turn, u, 1)
                        for w in range(v, v + ES):
                            if live(t2, w, -SL):
                                pool.wait_ge(gath_in[w], gathered(l, t2 - 1, w))
                        nc.gpsimd.tensor_copy(idx[:, v // ES, :], src_i[:, bass.ds((t2 * SL + v) * TQ, ES * TQ)])\
                            .then_inc(idx_set, 1)
                    if live(turn, u):
                        m = turn * SL + u + l * QUADS
                        freed = m - SL + 1
                        sets = turn * (SL // ES) + u // ES + 1 + l * IDX_SETS
                        if not isinstance(turn, int):
                            freed, sets = pool.to_reg(freed), pool.to_reg(sets)
                            pool.wait_ge(idx_in, IDX_LOADS)
                        if live(turn, u, -SL):
                            pool.wait_ge(z_ready, freed)
                        if u % ES == 0:
                            pool.wait_ge(idx_set, sets)
                        for k in range(TQ):
                            if isinstance(turn, int) and (SL * turn + u) * TQ + k >= FULL:
                                continue
                            nc.gpsimd.indirect_dma_start(
                                gath[:, u, k, :], None, b_table,
                                bass.IndirectOffsetOnAxis(ap=idx[:, u // ES, u % ES * TQ + k:u % ES * TQ + k + 1],
                                                          axis=0)).then_inc(gath_in[u], 16)

                def fast():
                    steps(pool, gather, 1, 0)

                def general():
                    pool.wait_ge(a_out, 16 * (l + 1) * len(STORES))

                    def indices(t, v):
                        nc.gpsimd.tensor_copy(idx[:, v, 0:1], dst_i[:, bass.ds(t, 1)]).then_inc(g_idx_set, 1)
                        nc.gpsimd.tensor_copy(idx[:, v, 1:2], src_i[:, bass.ds(t, 1)]).then_inc(g_idx_set, 1)

                    if l:
                        pool.wait_ge(g_idx_set, 2 * (TILES + 1))
                    indices(0, 0)
                    before = l * (TILES + 1)

                    def tiles(i):
                        for v in range(2):
                            t = i * 2 + v
                            m = t + l * TILES
                            if l or not isinstance(i, int) or v:
                                pool.wait_ge(g_z, m)
                            pool.wait_ge(g_idx_set, (t + before + 1) * 2)
                            indices(t + 1, 1 - v)
                            for k, table in enumerate((a_table, b_table)):
                                nc.gpsimd.indirect_dma_start(
                                    gath[:, 0, k, :], None, table,
                                    bass.IndirectOffsetOnAxis(ap=idx[:, v, k:k + 1], axis=0)).then_inc(g_rows_in, 16)

                    first_then_rest(pool, tiles, TILES // 2)

                if l == 0:
                    pool.wait_ge(flag_ready, 1)
                choose(pool, fast, general)
                if l == 0:
                    pool.wait_ge(inv_ready, 1)
                    nc.gpsimd.memset(acc[:, 1, :], 0.0).then_inc(acc_zero, 1)

        @block.tensor
        def _(pe):
            def copied_out(g):
                if g < DVE_GROUPS:
                    pe.wait_ge(h_t_ready, g + 1)
                else:
                    pe.wait_ge(h_t_ready_act, g - DVE_GROUPS + 1)

            pe.wait_ge(ident_ready, 1)
            for g in range(NG):
                if g < DVE_GROUPS:
                    pe.wait_ge(h_ready, g + 1)
                else:
                    pe.wait_ge(h_ready_act, g - DVE_GROUPS + 1)
                if g >= 3:
                    copied_out(g - 3)
                for k, c in enumerate(group(g)[0]):
                    t = nc.tensor.transpose(turn_bank[g % 3][:, k * P:(k + 1) * P], h_rows[:, c, :], ident[:])
                t.then_inc(turned, 1)
            pe.wait_ge(w_ready, 3)
            pe.wait_ge(iota_ready, 5)

            def fold(l):
                for g in range(NG):
                    if g >= 3 or l:
                        pe.wait_ge(out_ready, l * NG + g - 2)
                    for k, c in enumerate(group(g)[0]):
                        mm = nc.tensor.matmul(turn_bank[g % 3][:, k * P:(k + 1) * P], acc[:, l, c * P:(c + 1) * P],
                                              scales[:, l, :], start=True, stop=True)
                    mm.then_inc(fold_mm, 1)

            def ahead_product(c, slot):
                pe.wait_ge(h_part_ready, c + 1)
                to = ahead_bank[slot]
                nc.tensor.matmul(to[:, 0:2 * Z], h_part[:, slot, :],
                                 w_node[:, 1].rearrange("p s j f -> p (s j f)"), start=True, stop=False)
                nc.tensor.matmul(to[:, 0:Z], ones_row[:], bias[0:1, 1].rearrange("p j f -> p (j f)"),
                                 start=False, stop=True).then_inc(ahead_mm, 1)

            for l in range(2):
                if l:
                    pe.wait_ge(ahead_rows, CH)
                    pe.wait_ge(w_scaled, 1)
                for c in range(2 * CH):
                    s, c = (1, c) if c < CH else (0, c - CH)
                    if l == 0:
                        copied_out(c // 4)
                    if c >= TP:
                        pe.wait_ge((a_rows, b_rows)[s], l * CH + c - TP + 1)
                    elif s == 0:
                        pe.wait_ge(b_rows, (l + 1) * CH - TP + c + 1)
                    nc.tensor.matmul(bank[c % TP][:, 0:Z], (acc[:, 0] if l else h_t)[:, c * P:(c + 1) * P],
                                     w_node[:, 0, s, :, :].rearrange("p j f -> p (j f)"),
                                     start=True, stop=True).then_inc(tab_mm, 1)
                pe.wait_ge(a_rows, (l + 1) * CH)
                if l == 0:
                    pe.wait_ge(bn_ready, 1)
                    nc.tensor.matmul(ps_s[0][:, 0:P], hot_w[:], ident[:], start=True, stop=True)\
                        .then_inc(spread_mm, 1)
                    for c in range(AHEAD):
                        if c >= 2:
                            pe.wait_ge(ahead_rows, c - 1)
                        ahead_product(c, c % 2)
                    pe.wait_ge(base_ready, 2)
                else:
                    fold(0)
                    pe.wait_ge(out_ready, NG)

                def products(turn, u):
                    if live(turn, u):
                        m = turn * SL + u + l * QUADS
                        pe.wait_ge(hots_ready, m + 1)
                        pe.wait_ge(edge_in[u % ES], loads(l, turn, u))
                        pe.wait_ge(win_in[u % ES], loads(l, turn, u, GQ))
                        if live(turn, u, -2):
                            pe.wait_ge(z_ready, m - 1)
                        for k in range(TQ):
                            mm = nc.tensor.matmul(ps_z[u % 2][:, k, :], left[:, u % ES, k * P:(k + 1) * P],
                                                  right[:, u % ES, k // TG, :], start=True, stop=True)
                        mm.then_inc(z_mm, 1)
                    if live(turn, u, -2):
                        v = (u - 2) % SL
                        m = turn * SL + u - 2 + l * QUADS
                        pe.wait_ge(msg_ready, m + 1)
                        if live(turn, u, -4):
                            pe.wait_ge(acc_done, GQ * (m - 1))
                        sums = ps_s[v % 2][:, 0:GQ * 2 * W].rearrange("p (g s w) -> p g s w", g=GQ, s=2)
                        bits = hot[:, v, :, :].bitcast(BF16).rearrange("p t (w two) -> p t w two", two=2)
                        for g in range(GQ):
                            for k in range(TG):
                                mm = nc.tensor.matmul(sums[:, g, 0, :], msg[:, v % 2, g * TG + k, :],
                                                      hot[:, v, g * TG + k, :], start=k == 0, stop=k == TG - 1)
                            if l == 0:
                                for k in range(TG):
                                    mm = nc.tensor.matmul(sums[:, g, 1, :], ones_bf[:], bits[:, g * TG + k, :, 1],
                                                          start=k == 0, stop=k == TG - 1)
                        mm.then_inc(sums_mm, 1)
                    c = ahead_chunk(turn, u, 2)
                    if l == 0 and c is not None:
                        pe.wait_ge(ahead_rows, c)
                        ahead_product(c, 0)

                def fast():
                    steps(pe, products, 0, 2)

                def general():
                    def tile(t):
                        m = t + l * TILES
                        pe.wait_ge(g_edge_in, 16 * (m + 1))
                        if l or not isinstance(t, int):
                            pe.wait_ge(g_zb, m)
                        nc.tensor.matmul(ps_z[0][:, 0, :], left[W:P, 0, 0:P], right[W:P, 0, 0, :],
                                         start=True, stop=True).then_inc(g_z_mm, 1)
                        with pe.Fori(0, CH) as w:
                            pe.wait_ge(g_msg, m + 1)
                            pe.wait_ge(g_hot, m * CH + w + 1)
                            bits = hot_w[:].bitcast(BF16).rearrange("p (w two) -> p w two", two=2)
                            mm = nc.tensor.matmul(ps_s[0][:, 0:P], msg[:, 0, 0, :], hot_w[:],
                                                  start=True, stop=True)
                            if l == 0:
                                mm = nc.tensor.matmul(ps_s[0][:, P:2 * P], ones_bf[:], bits[:, :, 1],
                                                      start=True, stop=True)
                            mm.then_inc(g_sums, 1)

                    if l == 0:
                        with pe.Fori(AHEAD, CH) as c:
                            pe.wait_ge(ahead_rows, c)
                            ahead_product(c, 0)
                    first_then_rest(pe, tile, TILES)

                pe.wait_ge(right_ready, l + 1)
                if l == 0:
                    pe.wait_ge(flag_ready, 1)
                choose(pe, fast, general)

                pe.wait_ge(edges_done, l + 1)

            fold(1)

        @block.scalar
        def _(act):
            act.wait_ge(var_ready, 1)
            nc.scalar.activation(rstd[:], var[:], ACT.Sqrt).then_inc(root_ready, 1)
            act.wait_ge(var_ready, 2)
            nc.scalar.activation(bn_tmp[:, :, 1], bn_tmp[:, :, 0], ACT.Sqrt).then_inc(root_ready, 1)
            act.preload_act_table_set(LOG_EXP)
            act.wait_ge(shift_ready, 1)
            for g in range(DVE_GROUPS, NG):
                for c in group(g)[0]:
                    a = nc.scalar.activation(h_rows[:, c, :], x_rows[:, c, :], ACT.Relu,
                                             bias=shift[:, c:c + 1], scale=rstd[:, c:c + 1])
                a.then_inc(h_ready_act, 1)
            for g in range(DVE_GROUPS, NG):
                act.wait_ge(turned, g + 1)
                cols = group(g)[1]
                nc.scalar.copy(h_t[:, cols], turn_bank[g % 3][:, 0:cols.stop - cols.start]).then_inc(h_t_ready_act, 1)
            with act.Fori(0, TURN_N) as i:
                for u in range(TP):
                    act.wait_ge(tab_mm, i * TP + u + 1)
                    nc.scalar.copy(b_stage[:, bass.ds(i * TP + u, 1), :], bank[u][:, 0:Z].unsqueeze(1))\
                        .then_inc(b_rows, 1)
            act.wait_ge(bn_ready, 1)
            act.wait_ge(tab_mm, 2 * CH)
            nc.scalar.activation(w_node[:, 0], w_node[:, 1], ACT.Identity, scale=bn_scale[:, 0:1]).then_inc(w_scaled, 1)

            def ahead_part(c, slot):
                nc.scalar.activation(h_part[:, slot, :], h_t[:, bass.ds(c * P, P)], ACT.Identity,
                                     bias=bn_shift[:, 0:1]).then_inc(h_part_ready, 1)

            def ahead_copy(c, slot):
                act.wait_ge(ahead_mm, c + 1)
                nc.scalar.copy(node[:, bass.ds(c * 2 * Z, 2 * Z)], ahead_bank[slot][:, 0:2 * Z])\
                    .then_inc(ahead_rows, 1)

            act.wait_ge(base_ready, 1)
            for c in range(AHEAD + 1):
                if c < AHEAD:
                    if c >= 2:
                        act.wait_ge(ahead_mm, c - 1)
                    ahead_part(c, c % 2)
                if c:
                    ahead_copy(c - 1, (c - 1) % 2)

            for l in range(2):
                def logs(turn, u):
                    if live(turn, u, 4) and live(turn, u, 4 - ES):
                        t2, v = at(turn, u, 4)
                        act.wait_ge(hots_ready, t2 * SL + v + l * QUADS - ES + 1)
                        targets(nc.scalar, t2, v)
                    if not live(turn, u):
                        return
                    h = u % 2
                    m = turn * SL + u + l * QUADS
                    act.wait_ge(z_ready, m + 1)
                    if live(turn, u, -2):
                        act.wait_ge(soft_ready, m - 1)
                    nc.scalar.activation(lnz[:, h], z[:, h], ACT.Exp).then_inc(exp_ready, 1)
                    act.wait_ge(exp_ready, m + 1)
                    nc.scalar.activation(lnz[:, h], lnz[:, h], ACT.Ln, bias=1.0).then_inc(ln_ready, 1)
                    act.wait_ge(ln_ready, m + 1)
                    if live(turn, u, -2):
                        act.wait_ge(msg_ready, m - 1)
                    nc.scalar.activation(gate[:, h], lnz[:, h, :, 0:F], ACT.Exp, scale=-1.0).then_inc(gate_ready, 1)
                    if l == 0:
                        c = ahead_chunk(turn, u, 0)
                        if c is not None:
                            act.wait_ge(ahead_mm, c)
                            ahead_part(c, 0)
                        c = ahead_chunk(turn, u, 4)
                        if c is not None:
                            ahead_copy(c, 0)

                def fast():
                    steps(act, logs, 1, 0)

                def general():
                    def tile(t):
                        m = t + l * TILES
                        act.wait_ge(g_z, m + 1)
                        nc.scalar.activation(lnz[:, 0, 0], z[:, 0, 0], ACT.Exp).then_inc(g_exp, 1)
                        act.wait_ge(g_exp, m + 1)
                        nc.scalar.activation(lnz[:, 0, 0], lnz[:, 0, 0], ACT.Ln, bias=1.0).then_inc(g_ln, 1)
                        act.wait_ge(g_ln, m + 1)
                        nc.scalar.activation(gate[:, 0, 0], lnz[:, 0, 0, 0:F], ACT.Exp, scale=-1.0)\
                            .then_inc(g_gate, 1)

                    if l == 0:
                        with act.Fori(AHEAD, CH) as c:
                            act.wait_ge(ahead_mm, c)
                            ahead_part(c, 0)
                            ahead_copy(c, 0)
                    first_then_rest(act, tile, TILES)

                if l == 0:
                    act.wait_ge(flag_ready, 1)
                choose(act, fast, general)

        @block.vector
        def _(dve):
            done = [0]

            def link(ins):
                done[0] += 1
                ins.then_inc(prep, 1)
                dve.wait_ge(prep, done[0])

            for g in range(NG):
                dve.wait_ge(x_in[g], 16)
                for c in group(g)[0]:
                    st = nc.vector.bn_stats(stats[:, c, :], x_rows[:, c, :])
            link(st)
            mean_e, mean_o, m2_e, m2_o = stats[:, :, 1], stats[:, :, 4], stats[:, :, 2], stats[:, :, 5]
            nc.vector.tensor_tensor(mean[:], mean_e, mean_o, ALU.add)
            nc.vector.tensor_tensor(tmp[:], mean_e, mean_o, ALU.subtract)
            link(nc.vector.tensor_tensor(var[:], m2_e, m2_o, ALU.add))
            nc.vector.tensor_scalar(mean[:], mean[:], 0.5, None, ALU.mult)
            link(nc.vector.tensor_tensor(tmp[:], tmp[:], tmp[:], ALU.mult))
            link(nc.vector.scalar_tensor_tensor(var[:], tmp[:], F / 4.0, var[:], ALU.mult, ALU.add))
            nc.vector.tensor_scalar(var[:], var[:], 1.0 / F, LN_EPS, ALU.mult, ALU.add).then_inc(var_ready, 1)
            dve.wait_ge(w_in, W_LOADS)
            nc.vector.tensor_scalar(bn_tmp[:, :, 0], bn[:, :, 3], BN_EPS, None, ALU.add).then_inc(var_ready, 1)
            dve.wait_ge(root_ready, 1)
            link(nc.vector.reciprocal(rstd[:], rstd[:]))
            nc.vector.scalar_tensor_tensor(shift[:], mean[:], -1.0, rstd[:], ALU.mult, ALU.mult)\
                .then_inc(shift_ready, 1)
            for g in range(DVE_GROUPS + 2):
                if g < DVE_GROUPS:
                    for c in group(g)[0]:
                        nrm = nc.vector.tensor_scalar(h_rows[:, c, :], x_rows[:, c, :], mean[:, c:c + 1],
                                                      rstd[:, c:c + 1], ALU.subtract, ALU.mult)
                    nrm.then_inc(h_ready, 1)
                if g >= 2:
                    dve.wait_ge(turned, g - 1)
                    cols = group(g - 2)[1]
                    nc.vector.tensor_scalar(h_t[:, cols], turn_bank[(g - 2) % 3][:, 0:cols.stop - cols.start],
                                            0.0, None, ALU.max).then_inc(h_t_ready, 1)

            dve.wait_ge(root_ready, 2)
            link(nc.vector.reciprocal(bn_tmp[:, :, 1], bn_tmp[:, :, 1]))
            link(nc.vector.tensor_tensor(bn_scale[:], bn[:, :, 0], bn_tmp[:, :, 1], ALU.mult))
            link(nc.vector.tensor_tensor(bn_tmp[:, :, 0], bn[:, :, 2], bn_scale[:], ALU.mult))
            link(nc.vector.tensor_tensor(bn_shift[:], bn[:, :, 1], bn_tmp[:, :, 0], ALU.subtract))
            link(nc.vector.tensor_tensor(shift_sum[:], bn_shift[:, 0:1], bn_shift[:, 1:2], ALU.add))
            dve.wait_ge(ident_ready, 1)
            for l in range(2):
                nc.vector.tensor_scalar(scales[:, l, :], ident[:], bn_scale[:, l:l + 1], None, ALU.mult)
            nc.vector.tensor_scalar(hot_w[:], ident[:], 0.0, shift_sum[:], ALU.mult, ALU.add).then_inc(bn_ready, 1)

            dve.wait_ge(idx_in, IDX_LOADS)
            dve.wait_ge(iota_ready, 5)
            nc.vector.tensor_copy(iota_f[:], iota_i[:])
            nc.vector.tensor_copy(part_f[:], part_i[:])
            nc.vector.tensor_copy(first_f[:], first_i[:])
            link(nc.vector.tensor_copy(dst_f[:], dst_i[:, 0:TILES]))
            nc.vector.tensor_scalar(target[:], first_f[0:W, :], part_f[0:W, :], None, ALU.add)
            link(nc.vector.tensor_tensor(rel[:].rearrange("p (g t) -> p g t", t=TG),
                                         dst_f[:].rearrange("p (g t) -> p g t", t=TG),
                                         first_f[:].unsqueeze(2).to_broadcast((P, GROUPS, TG)), ALU.subtract))
            link(nc.vector.tensor_scalar(outside[:], rel[:], 0.0, None, ALU.is_lt))
            link(nc.vector.scalar_tensor_tensor(outside2[:], rel[:], W - 1.0, outside[:], ALU.is_gt, ALU.max))
            nc.vector.tensor_reduce(worst[:], outside2[:], AX.X, ALU.max).then_inc(worst_ready, 1)

            dve.wait_ge(worst_spread, 1)
            nc.vector.tensor_copy(flag[:], worst_all[:]).then_inc(flag_ready, 1)

            dve.wait_ge(h_ready, DVE_GROUPS)
            dve.wait_ge(h_ready_act, ACT_GROUPS)
            nc.vector.scalar_tensor_tensor(x_rows[:], h_rows, 0.0, x_rows[:], ALU.max, ALU.add).then_inc(base_ready, 1)

            def fold(l):
                for g in range(NG):
                    dve.wait_ge(fold_mm, l * NG + g + 1)
                    for k, c in enumerate(group(g)[0]):
                        add = nc.vector.scalar_tensor_tensor(
                            x_rows[:, c, :], turn_bank[g % 3][:, k * P:(k + 1) * P], inv[:, c:c + 1], x_rows[:, c, :],
                            ALU.mult, ALU.add)
                    add.then_inc(out_ready, 1)

            def edge_weights(l):
                for j in range(ES):
                    mv = nc.vector.tensor_copy(
                        right[W:P, j], w_edge[W:P, l].rearrange("p j f -> p (j f)").unsqueeze(1)
                        .to_broadcast((FE, GQ, Z)))
                mv.then_inc(right_ready, 1)

            dve.wait_ge(w_ready, 3)
            edge_weights(0)
            for l in range(2):
                if l == 0:
                    with dve.Fori(0, TURN_N) as i:
                        for u in range(TP):
                            dve.wait_ge(tab_mm, CH + i * TP + u + 1)
                            nc.vector.tensor_tensor(a_stage[:, bass.ds(i * TP + u, 1), :],
                                                    bank[u][:, 0:Z].unsqueeze(1),
                                                    bias[:, l].rearrange("p j f -> p (j f)").unsqueeze(1),
                                                    ALU.add).then_inc(a_rows, 1)
                    dve.wait_ge(spread_mm, 1)
                    dve.wait_ge(base_ready, 1)
                    nc.vector.tensor_tensor(x_rows[:], x_rows[:],
                                            ps_s[0][:, 0:P].unsqueeze(1).to_broadcast((P, CH, F)), ALU.add)\
                        .then_inc(base_ready, 1)
                else:
                    dve.wait_ge(ahead_rows, CH)

                    for a in range(0, P, SQ):
                        nodes = acc[a:a + SQ, 1, :].rearrange("p (c q) -> p c q", q=P)
                        turn = nc.vector.transpose(squares[a:a + SQ], nodes[:, :, a:a + SQ])
                    link(turn)
                    link(nc.vector.tensor_scalar(edges_col[:], squares[:, :, 0], 1.0, None, ALU.max))
                    nc.vector.reciprocal(inv[:], edges_col[:]).then_inc(inv_ready, 1)
                    dve.wait_ge(inv_ready, 1)

                    for s, rows_ready in ((1, b_rows), (0, a_rows)):
                        for c in range(CH):
                            dve.wait_ge(tab_mm, (3 - s) * CH + c + 1)
                            nc.vector.scalar_tensor_tensor(ahead[:, c, s, :], bank[c % TP][:, 0:Z], inv[:, c:c + 1],
                                                           ahead[:, c, s, :], ALU.mult, ALU.add)\
                                .then_inc(rows_ready, 1)
                    edge_weights(1)
                    dve.wait_ge(base_ready, 2)
                    fold(0)
                dve.wait_ge(acc_zero, l + 1)

                def elementwise(turn, u):
                    if live(turn, u):
                        h = u % 2
                        m = turn * SL + u + l * QUADS
                        dve.wait_ge(z_mm, m + 1)
                        dve.wait_ge(gath_in[u], gathered(l, turn, u))
                        if live(turn, u, -2):
                            dve.wait_ge(soft_ready, m - 1)
                        nc.vector.tensor_tensor(z[:, h], ps_z[h][:], gath[:, u], ALU.add).then_inc(z_ready, 1)
                    if live(turn, u, -2):
                        rows = [first_row(dve, (turn * SL + u - 2) * GQ + g) for g in range(GQ)]
                    if live(turn, u, -1):
                        h = (u - 1) % 2
                        m = turn * SL + u - 1 + l * QUADS
                        dve.wait_ge(ln_ready, m + 1)
                        if live(turn, u, -3):
                            dve.wait_ge(msg_ready, m - 1)
                        nc.vector.scalar_tensor_tensor(soft[:, h], lnz[:, h, :, F:Z], CAP, z[:, h, :, F:Z],
                                                       ALU.min, ALU.max).then_inc(soft_ready, 1)
                    if live(turn, u, -1):
                        h = (u - 1) % 2
                        m = turn * SL + u - 1 + l * QUADS
                        dve.wait_ge(gate_ready, m + 1)
                        dve.wait_ge(soft_ready, m + 1)
                        if live(turn, u, -3):
                            dve.wait_ge(sums_mm, m - 1)
                        nc.vector.tensor_tensor(msg[:, h], gate[:, h], soft[:, h],
                                                ALU.mult).then_inc(msg_ready, 1)
                    for g in range(GQ):
                        if live(turn, u, -2):
                            h = u % 2
                            m = turn * SL + u - 2 + l * QUADS
                            if g == 0:
                                dve.wait_ge(sums_mm, m + 1)
                            if live(turn, u, -3) or g:
                                dve.wait_ge(acc_done, GQ * m + g)
                            sums = ps_s[h][:, 0:GQ * 2 * W].rearrange("p (g s w) -> p g s w", g=GQ, s=2)
                            k = 2 - l
                            there = acc[:, l:l + k, bass.ds(rows[g], W)]
                            nc.vector.tensor_tensor(there, there, sums[:, g, 0:k, :], ALU.add).then_inc(acc_done, 1)
                        if live(turn, u, 2):
                            t2, v = at(turn, u, 2)
                            n = t2 * SL + v
                            m = n + l * QUADS
                            if g == 0:
                                dve.wait_ge(dst_in[v % ES], loads(l, t2, v))
                                if live(t2, v, -ES):
                                    dve.wait_ge(z_mm, m - ES + 1)
                                if live(t2, v, -SL):
                                    dve.wait_ge(sums_mm, m - SL + 1)
                            part = slice(g * TG * P, (g + 1) * TG * P)
                            nc.vector.tensor_scalar(left[0:W, v % ES, part], dst_b[:, v % ES, part],
                                                    target[:, bass.ds(n * GQ + g, 1)], None, ALU.is_equal)
                            if g == GQ - 1:
                                nc.vector.tensor_tensor(
                                    hot[:, v], iota_f[:, 0:W].unsqueeze(1).to_broadcast((P, TQ, W)),
                                    rel[:, bass.ds(n * TQ, TQ)].unsqueeze(2).to_broadcast((P, TQ, W)),
                                    ALU.is_equal).then_inc(hots_ready, 1)

                def fast():
                    steps(dve, elementwise, 2, 2)
                    dve.wait_ge(acc_done, GQ * QUADS * (l + 1))
                    dve.sem_inc(edges_done, 1)

                def general():
                    def tile(t):
                        m = t + l * TILES
                        dve.wait_ge(g_z_mm, m + 1)
                        dve.wait_ge(g_rows_in, 32 * (m + 1))
                        nc.vector.tensor_tensor(z[:, 0, 0], ps_z[0][:, 0], gath[:, 0, 0], ALU.add).then_inc(g_zb, 1)
                        dve.wait_ge(g_zb, m + 1)
                        nc.vector.tensor_tensor(z[:, 0, 0], z[:, 0, 0], gath[:, 0, 1], ALU.add).then_inc(g_z, 1)
                        dve.wait_ge(g_ln, m + 1)
                        nc.vector.scalar_tensor_tensor(soft[:, 0, 0], lnz[:, 0, 0, F:Z], CAP, z[:, 0, 0, F:Z],
                                                       ALU.min, ALU.max).then_inc(g_soft, 1)
                        nc.vector.tensor_copy(rel_w[:], dst_f[:, bass.ds(t, 1)]).then_inc(g_rel, 1)
                        dve.wait_ge(g_gate, m + 1)
                        dve.wait_ge(g_soft, m + 1)
                        if l or not isinstance(t, int):
                            dve.wait_ge(g_acc, m * CH)
                        nc.vector.tensor_tensor(msg[:, 0, 0], gate[:, 0, 0], soft[:, 0, 0],
                                                ALU.mult).then_inc(g_msg, 1)
                        with dve.Fori(0, CH) as w:
                            dve.wait_ge(g_rel, m * (CH + 1) + w + 1)
                            nc.vector.tensor_scalar(hot_w[:], iota_f[:], rel_w[:], None, ALU.is_equal)\
                                .then_inc(g_hot, 1)
                            dve.wait_ge(g_hot, m * CH + w + 1)
                            nc.vector.tensor_scalar(rel_w[:], rel_w[:], -float(P), None, ALU.add).then_inc(g_rel, 1)
                            dve.wait_ge(g_sums, m * CH + w + 1)
                            k = 2 - l
                            there = acc[:, l:l + k, bass.ds(w * P, P)]
                            nc.vector.tensor_tensor(
                                there, there, ps_s[0][:, 0:k * P].rearrange("p (s w) -> p s w", s=k),
                                ALU.add).then_inc(g_acc, 1)

                    first_then_rest(dve, tile, TILES)
                    dve.wait_ge(g_acc, CH * TILES * (l + 1))
                    dve.sem_inc(edges_done, 1)

                if l == 0:
                    dve.wait_ge(flag_ready, 1)
                choose(dve, fast, general)

            dve.wait_ge(out_ready, NG)
            fold(1)


_WEIGHTS = [f"{n}{l}" for l in (1, 2) for n in ("Wf", "bf", "Ws", "bs", "gamma", "beta", "rmean", "rvar")]


def kernel(**inputs):
    import concourse.bacc as bacc
    from concourse.bass_utils import run_bass_kernel_spmd

    x = np.zeros((NP, F), np.float32)
    x[:N_NODES] = np.asarray(inputs["x"])
    src = np.zeros((EP,), np.int32)
    src[:N_EDGES] = np.asarray(inputs["src"])
    dst = np.full((EP,), N_NODES, np.int32)
    dst[:N_EDGES] = np.asarray(inputs["dst"])
    edge = np.zeros((EP, FE), np.float32)
    edge[:N_EDGES] = np.asarray(inputs["edge_attr_64"])
    cols = np.zeros((2, P, COLS), np.int32)
    cols[0, :, :TILES] = src.reshape(TILES, P).T
    cols[1, :, :TILES] = dst.reshape(TILES, P).T
    arrays = {
        "x": x,
        "src_cols": cols[0],
        "dst_cols": cols[1],
        "dst_row": dst,
        "dst_first": np.ascontiguousarray(dst[::TG * P]),
        "edge_t": np.ascontiguousarray(edge.T),
    }
    w = {n: np.asarray(inputs[f"L0_gnn_{n}"]) for n in _WEIGHTS}
    both = [np.concatenate([w[f"Wf{l}"], w[f"Ws{l}"]], axis=1) for l in (1, 2)]
    arrays["w_node_in"] = np.ascontiguousarray(
        np.concatenate([b[a:a + F] for b in both for a in (0, F)], axis=1))
    arrays["w_edge_in"] = np.ascontiguousarray(np.concatenate([b[2 * F:] for b in both], axis=1))
    arrays["bias_in"] = np.concatenate([w[f"{n}{l}"] for l in (1, 2) for n in ("bf", "bs")])
    arrays["bn_in"] = np.ascontiguousarray(
        np.stack([w[f"{n}{l}"] for l in (1, 2) for n in ("gamma", "beta", "rmean", "rvar")], axis=1))

    nc = bacc.Bacc("TRN2", target_bir_lowering=False, num_devices=1)
    aps = {n: nc.dram_tensor(f"in_{n}", a.shape, mybir.dt.from_np(a.dtype), kind="ExternalInput").ap()
           for n, a in arrays.items()}
    out = nc.dram_tensor("out", (N_NODES, F), F32, kind="ExternalOutput").ap()
    build(nc, out=out, **aps)
    r = run_bass_kernel_spmd(nc, [{f"in_{n}": a for n, a in arrays.items()}], core_ids=[0])
    return r.results[0]["out"]
```
